# Optimizing a Trainium2 kernel written in Bass

```python
import numpy as np
import jax
import jax.numpy as jnp

def _softmax(x, axis=-1):
    return jax.nn.softmax(x, axis=axis)

def _gelu(x):
    return jax.nn.gelu(x, approximate=True)

def _silu(x):
    return jax.nn.silu(x)

def _sigmoid(x):
    return jax.nn.sigmoid(x)

def _layernorm(x, axis=-1, eps=1e-05):
    m = jnp.mean(x, axis=axis, keepdims=True)
    v = jnp.var(x, axis=axis, keepdims=True)
    return (x - m) / jnp.sqrt(v + eps)

def _scatter_add(tgt, idx, src, axis=0):
    return tgt.at[idx].add(src)

def _segment_sum(src, seg, n):
    return jax.ops.segment_sum(src, seg, n)
kernel_name = 'mk_adj_ffn_d1_adj_r2_e9e28b'

def setup_inputs(seed: int=0):
    np.random.seed(seed)
    _w = jnp.asarray

    def _rec_inputs():
        import jax
        import jax.numpy as jnp
        _gk = jax.random.key(seed)
        x = -0.0002928 + 1 * jax.random.normal(jax.random.fold_in(_gk, 1), (4096, 128), jnp.float32)
        _a = jax.random.bernoulli(jax.random.fold_in(_gk, 2), 0.000976562, (4096, 4096))
        _a = jnp.logical_or(_a, jnp.swapaxes(_a, -1, -2))
        _a = jnp.logical_or(_a, jnp.eye(4096, dtype=bool))
        adj = _a.astype(jnp.int32)
        return (x, adj)
    x, adj = _rec_inputs()

    def _L0_gnn_setup():
        import jax, jax.numpy as jnp
        import numpy as np
        N = 8192
        F_IN = 128
        F_OUT = 128
        key = jax.random.key(seed)
        k1, k2, k3 = jax.random.split(key, 3)
        x = jax.random.normal(k1, (N, F_IN), dtype=jnp.float32)
        adj = jax.random.randint(k2, (N, N), 0, 2, dtype=jnp.int32)
        stdv = np.sqrt(6.0 / (2 * F_IN + F_OUT)).astype(np.float32)
        weight = jax.random.uniform(k3, (2 * F_IN, F_OUT), dtype=jnp.float32, minval=-stdv, maxval=stdv)
        bias = jnp.zeros((F_OUT,), dtype=jnp.float32)
        return {'x': x, 'adj': adj, 'weight': weight, 'bias': bias}
    _L0_gnn_all = _L0_gnn_setup()
    _L0_gnn_in = {k: v for k, v in _L0_gnn_all.items() if k in ('weight', 'bias')}
    del _L0_gnn_all

    def _L0_ffn_setup():
        import math
        import jax, jax.numpy as jnp
        import numpy as np
        CAPACITY_FACTOR = 1.25
        TOP_K = 2
        LN_EPS = 1e-05

        def _layer_norm(x, gamma, beta):
            mu = jnp.mean(x, axis=-1, keepdims=True)
            var = jnp.var(x, axis=-1, keepdims=True)
            return (x - mu) * jax.lax.rsqrt(var + LN_EPS) * gamma + beta
        key = jax.random.key(seed)
        ks = jax.random.split(key, 4)
        B, S, D, F, E = (8, 2048, 128, 256, 8)
        x = jax.random.normal(ks[0], (B, S, D), dtype=jnp.float32)
        Wr = jax.random.normal(ks[1], (D, E), dtype=jnp.float32) / np.sqrt(D)
        br = jnp.zeros((E,), jnp.float32)
        W1 = jax.random.normal(ks[2], (E, D, F), dtype=jnp.float32) / np.sqrt(D)
        b1 = jnp.zeros((E, F), jnp.float32)
        W2 = jax.random.normal(ks[3], (E, F, D), dtype=jnp.float32) / np.sqrt(F)
        b2 = jnp.zeros((E, D), jnp.float32)
        gamma = jnp.ones((D,), jnp.float32)
        beta = jnp.zeros((D,), jnp.float32)
        return {'x': x, 'Wr': Wr, 'br': br, 'W1': W1, 'b1': b1, 'W2': W2, 'b2': b2, 'gamma': gamma, 'beta': beta}
    _L0_ffn_all = _L0_ffn_setup()
    _L0_ffn_in = {k: v for k, v in _L0_ffn_all.items() if k in ('Wr', 'br', 'W1', 'b1', 'W2', 'b2', 'gamma', 'beta')}
    del _L0_ffn_all
    return {'x': x, 'adj': adj, 'L0_gnn_weight': _L0_gnn_in['weight'], 'L0_gnn_bias': _L0_gnn_in['bias'], 'L0_ffn_Wr': _L0_ffn_in['Wr'], 'L0_ffn_br': _L0_ffn_in['br'], 'L0_ffn_W1': _L0_ffn_in['W1'], 'L0_ffn_b1': _L0_ffn_in['b1'], 'L0_ffn_W2': _L0_ffn_in['W2'], 'L0_ffn_b2': _L0_ffn_in['b2'], 'L0_ffn_gamma': _L0_ffn_in['gamma'], 'L0_ffn_beta': _L0_ffn_in['beta']}

def reference(x, adj, L0_gnn_weight, L0_gnn_bias, L0_ffn_Wr, L0_ffn_br, L0_ffn_W1, L0_ffn_b1, L0_ffn_W2, L0_ffn_b2, L0_ffn_gamma, L0_ffn_beta):
    import jax
    import jax.numpy as jnp

    def _L0_gnn_ref(x, adj, weight, bias):
        import jax, jax.numpy as jnp
        import numpy as np
        N = 8192
        F_IN = 128
        F_OUT = 128
        a = adj.astype(x.dtype)
        deg = jnp.sum(a, axis=1, keepdims=True)
        x1 = a @ x / deg
        n_x = jnp.concatenate([x1, x], axis=1)
        return n_x @ weight + bias

    def _L0_ffn_ref(x, Wr, br, W1, b1, W2, b2, gamma, beta):
        import math
        import jax, jax.numpy as jnp
        import numpy as np
        CAPACITY_FACTOR = 1.25
        TOP_K = 2
        LN_EPS = 1e-05

        def _layer_norm(x, gamma, beta):
            mu = jnp.mean(x, axis=-1, keepdims=True)
            var = jnp.var(x, axis=-1, keepdims=True)
            return (x - mu) * jax.lax.rsqrt(var + LN_EPS) * gamma + beta
        B, S, D = x.shape
        E = Wr.shape[1]
        N = B * S
        K = TOP_K
        logits = jnp.mean(x, axis=1) @ Wr + br
        routing_weights = jax.nn.softmax(logits, axis=-1)
        capacity = float(math.ceil(N * CAPACITY_FACTOR / E))
        expected_loads = routing_weights.sum(axis=0) * (N / B)
        scale = jnp.where(expected_loads > capacity, capacity / expected_loads, 1.0)
        routing_weights = jax.nn.softmax(routing_weights * scale, axis=-1)
        rw_tok = jnp.broadcast_to(routing_weights[:, None, :], (B, S, E)).reshape(N, E)
        top_w, top_i = jax.lax.top_k(rw_tok, K)
        top_w = jax.nn.softmax(top_w, axis=-1)
        xf = x.reshape(N, D)
        h = jax.nn.gelu(jnp.einsum('nd,edf->enf', xf, W1) + b1[:, None, :], approximate=False)
        y = jnp.einsum('enf,efd->end', h, W2) + b2[:, None, :]
        w_dense = jnp.zeros((N, E), x.dtype).at[jnp.arange(N)[:, None], top_i].add(top_w)
        out = jnp.einsum('ne,end->nd', w_dense, y).reshape(B, S, D)
        out = _layer_norm(out + x, gamma, beta)
        return out
    x = x + _L0_gnn_ref(_layernorm(x, axis=-1), adj, L0_gnn_weight, L0_gnn_bias)
    x = x + _L0_ffn_ref(_layernorm(x, axis=-1)[None], L0_ffn_Wr, L0_ffn_br, L0_ffn_W1, L0_ffn_b1, L0_ffn_W2, L0_ffn_b2, L0_ffn_gamma, L0_ffn_beta)[0]
    return x

_drawn_inputs = setup_inputs


def setup_inputs(seed=0):
    import zlib

    import numpy as np

    out = dict(_drawn_inputs(seed))
    spreads = {'L0_gnn_bias': (0.0, 0.1),
     'L0_ffn_br': (0.0, 0.8),
     'L0_ffn_b1': (0.0, 0.426),
     'L0_ffn_b2': (0.0, 0.323),
     'L0_ffn_gamma': (1.0, 0.2),
     'L0_ffn_beta': (0.0, 0.1)}
    factors = {'L0_ffn_Wr': 8.0}
    for name, (base, spread) in spreads.items():
        noise = np.random.default_rng([zlib.crc32(name.encode()), seed]).standard_normal(out[name].shape)
        drawn = base * np.exp(spread * noise) if base else spread * noise
        out[name] = jnp.asarray(drawn.astype(out[name].dtype))
    for name, factor in factors.items():
        out[name] = (out[name] * factor).astype(out[name].dtype)
    return out
```

```python
import math
from contextlib import ExitStack

import concourse.bass as bass
from concourse import mybir
from concourse.alu_op_type import AluOpType as ALU

F32 = mybir.dt.float32
F16 = mybir.dt.float16
I32 = mybir.dt.int32
U32 = mybir.dt.uint32
ACT = mybir.ActivationFunctionType
AX = mybir.AxisListType


def gnn_moe_kernel(nc, x, adj, gnn_weight, gnn_bias, Wr, br, W1, b1, W2, b2, gamma, beta, out):
    P = 128
    Q, L = 4, 32
    N, D = x.shape
    E, _, F = W1.shape
    T = N // P
    QS = N // Q
    NB = T // 2
    BR = QS // NB
    SPLIT = 4096.0
    EPS = 1e-5
    CAPACITY = float(math.ceil(N * 1.25 / E))
    TOPK = 2
    NC = F // P
    HC = TOPK * NC
    TC = 4
    NF = T // TC
    FW = TC * P
    PEEL = 4

    with ExitStack() as ctx:
        def sb(name, shape, dt=F32):
            return ctx.enter_context(nc.sbuf_tensor(name, shape, dt))

        def sem(name):
            return ctx.enter_context(nc.semaphore(name))

        adj_raw = [sb(f"adj_raw{s}", [P, Q, 2, QS], I32) for s in range(2)]
        adj_pair = sb("adj_pair", [P, Q, QS, 2], F16)
        adj_t = [sb(f"adj_t{s}", [P, Q, L, 2 * L], F16) for s in range(2)]
        deg_part = [sb(f"deg_part{s}", [P, Q, 2]) for s in range(2)]
        deg_spread = [sb(f"deg_spread{s}", [P, 2, Q, L // 2, 2]) for s in range(2)]
        xs_parts = sb("xs_parts", [P, T, 2, D], F16)
        x_res = sb("x_res", [P, T, D])
        xs = sb("xs", [P, T, D])
        xn_t = sb("xn_t", [P, T * P])
        w1_all = sb("w1_all", [P, E * F])
        b1_rows = sb("b1_rows", [E * NC, P])
        b1_all = sb("b1_all", [P, E * NC])
        wg = sb("wg", [P, 2, D])
        bg_row = sb("bg_row", [1, D])
        wr = sb("wr", [P, E])
        br_all = sb("br_all", [P, E])
        gamma_all = sb("gamma_all", [P, D])
        beta_all = sb("beta_all", [P, D])
        ident = sb("ident", [P, P])
        lane_mask = sb("lane_mask", [P, L])
        split_const = sb("split_const", [P, P])
        neg_half = sb("neg_half", [P, 8])
        eps_const = sb("eps_const", [P, TC])
        bn6 = sb("bn6", [P, T, 6])
        mv1 = sb("mv1", [P, T, 2])
        rstd1 = sb("rstd1", [P, T])
        bn6b = sb("bn6b", [P, 2, 6])
        xs_stage = [sb(f"xs_stage{s}", [P, 2, D]) for s in range(2)]
        x2_stage = [sb(f"x2_stage{s}", [P, 2, D]) for s in range(2)]
        xn_stage = [sb(f"xn_stage{s}", [P, 2, D]) for s in range(2)]
        mv2 = [sb(f"mv2_{s}", [P, 2, 2]) for s in range(2)]
        var2 = sb("var2", [P, 2])
        rstd2 = [sb(f"rstd2_{s}", [P, 2]) for s in range(2)]
        rdeg = sb("rdeg", [P, 2])
        agg_sb = sb("agg_sb", [P, 2 * P])
        xs_t = sb("xs_t", [P, 2 * P])
        col_sum = sb("col_sum", [P, NB])
        route = sb("route", [P, 24, E])
        top_idx = sb("top_idx", [P, 8], U32)
        b1_sel = sb("b1_sel", [P, TOPK, NC])
        b2_sel = sb("b2_sel", [P, D])
        free2 = adj_pair[:, :, :, :].rearrange("p k s e -> p (k s e)").bitcast(F32)
        w1_sel = free2[:, 0:TOPK * F]
        w2_sel = free2[:, TOPK * F:TOPK * F + HC * D].rearrange("p (k d) -> p k d", k=HC)
        free = adj_raw[0][:, :, :, :].rearrange("p k e s -> p (k e s)").bitcast(F32)
        hid = [[free[:, (s * HC + k) * FW:(s * HC + k + 1) * FW] for k in range(HC)] for s in range(2)]
        w2_all = free[:, 2 * HC * FW:2 * HC * FW + E * NC * D].rearrange("p (k d) -> p k d", k=E * NC)
        b2_all = free[:, 2 * HC * FW + E * NC * D:2 * HC * FW + E * NC * D + E * D]
        free1 = adj_raw[1][:, :, :, :].rearrange("p k e s -> p (k e s)").bitcast(F32)

        def slots(n):
            return [free1[:, (n + s) * FW:(n + s + 1) * FW].rearrange("p (t d) -> p t d", t=TC) for s in range(2)]
        skip, ysum, centred, result = slots(0), slots(2), slots(4), slots(6)
        bn6c = [sb(f"bn6c{s}", [P, TC, 6]) for s in range(2)]
        mv3 = [sb(f"mv3_{s}", [P, TC, 2]) for s in range(2)]
        var3 = [sb(f"var3_{s}", [P, TC]) for s in range(2)]
        rstd3 = [sb(f"rstd3_{s}", [P, TC]) for s in range(2)]

        bank = [ctx.enter_context(nc.psum_tensor(f"bank{i}", [P, 512], F32)) for i in range(8)]
        p_agg = [bank[0], bank[1]]
        p_xst, p_xnt, p_nb, p_self, p_deg = bank[2], bank[3], bank[4], bank[5], bank[6]
        p_logit = bank[7]

        x_in = sem("x_in")
        weights_in = sem("weights_in")
        eps_set = sem("eps_set")
        late_in = sem("late_in")
        self_staged = sem("self_staged")
        xn2_kept = sem("xn2_kept")
        adj_in = [[sem(f"adj_in{s}_{k}") for k in range(Q)] for s in range(2)]
        consts_done = sem("consts_done")
        pool_step = sem("pool_step")
        bn1_done = sem("bn1_done")
        stats1_done = sem("stats1_done")
        rstd1_done = sem("rstd1_done")
        norm1_done = sem("norm1_done")
        high_done = sem("high_done")
        low_done = sem("low_done")
        cast_done = sem("cast_done")
        turned = sem("turned")
        spread_done = sem("spread_done")
        agg_done = sem("agg_done")
        xst_done = sem("xst_done")
        agg_copied = sem("agg_copied")
        proj_done = sem("proj_done")
        self_added = sem("self_added")
        x2_done = sem("x2_done")
        bn2_done = sem("bn2_done")
        stats2_done = sem("stats2_done")
        var2_done = sem("var2_done")
        rstd2_done = sem("rstd2_done")
        norm2_done = sem("norm2_done")
        xnt_done = sem("xnt_done")
        xnt_copied = sem("xnt_copied")
        beta_added = sem("beta_added")
        chain = sem("chain")
        wr_scaled = sem("wr_scaled")
        b1_turned = sem("b1_turned")
        logits_done = sem("logits_done")
        exp_asked = sem("exp_asked")
        exp_done = sem("exp_done")
        sel_done = sem("sel_done")
        hid_mm_done = sem("hid_mm_done")
        gelu_done = sem("gelu_done")
        y_mm_done = sem("y_mm_done")
        skip_done = sem("skip_done")
        ysum_done = sem("ysum_done")
        bn3_done = sem("bn3_done")
        stats3_done = sem("stats3_done")
        var3_done = sem("var3_done")
        rstd3_done = sem("rstd3_done")
        centred_done = sem("centred_done")
        result_done = sem("result_done")
        stored = [sem(f"stored{s}") for s in range(2)]

        x_q = x.rearrange("(q b a) f -> q a b f", q=Q, b=T, a=L)
        out_q = out.rearrange("(q b a) f -> q a b f", q=Q, b=T, a=L)
        adj_v = adj.rearrange("(k n c e) (q s) -> n k q c e s", k=Q, n=NB, c=L, e=2, q=Q)

        block = ctx.enter_context(nc.Block())

        def live(b):
            return not isinstance(b, int) or 0 <= b < NB

        def load_adj(eng, b, s, quadrants):
            for k in range(Q):
                for q in quadrants:
                    eng.dma_start(adj_raw[s][32 * q:32 * q + 32, k, :, :], adj_v[b, k, q]).then_inc(adj_in[s][k], 16)

        @block.sync
        def _(sp):
            for q in range(Q):
                sp.dma_start(x_res[32 * q:32 * q + 32, :, :], x_q[q]).then_inc(x_in, 16)
            for s in range(2):
                load_adj(sp, s, s, (0, 1))
            with sp.Fori(2, NB - 1, 2) as b0:
                for s in range(2):
                    b = b0 + s
                    sp.wait_ge(cast_done, 8 * b - 8)
                    load_adj(sp, b, s, (0, 1))
            for f in range(NF):
                sp.wait_ge(result_done, TC * (f + 1))
                for q in range(Q):
                    sp.dma_start(out_q[q][:, TC * f:TC * f + TC, :], result[f % 2][32 * q:32 * q + 32, :, :])\
                      .then_inc(stored[f % 2], 16)
            for s in range(2):
                sp.wait_ge(stored[s], 16 * Q * NF // 2)

        @block.scalar
        def _(act):
            for s in range(2):
                load_adj(act, s, s, (2, 3))
            for g in range(4):
                act.wait_ge(norm1_done, 8 * (g + 1))
                act.activation(xs_parts[:, 8 * g:8 * g + 8, 0, :], xs[:, 8 * g:8 * g + 8, :], ACT.Copy)\
                   .then_inc(high_done, 1)

            def step(g, s):
                if live(g):
                    if not isinstance(g, int) or g >= 2:
                        act.wait_ge(spread_done, 2 * g - 2)
                    for k in range(Q):
                        act.wait_ge(adj_in[s][k], 32 * (g - s) + 64)
                        if not isinstance(g, int) or g >= 1:
                            act.wait_ge(turned, 4 * g - 3 + k)
                        for e in range(2):
                            act.activation(adj_pair[:, k, :, e], adj_raw[s][:, k, e, :], ACT.Copy,
                                           accum_out=deg_part[s][:, k, e:e + 1]).then_inc(cast_done, 1)
                if live(g - 3):
                    b = g - 3
                    act.wait_ge(xnt_done, b + 1)
                    act.activation(xn_t[:, bass.ds(b * 2 * P, 2 * P)], p_xnt[:, 0:2 * P], ACT.Copy,
                                   accum_out=col_sum[:, bass.ds(b, 1)]).then_inc(xnt_copied, 1)
                if live(g - 1):
                    b = g - 1
                    if not isinstance(b, int) or b >= 1:
                        act.wait_ge(proj_done, b)
                    act.wait_ge(agg_done, b + 1)
                    act.activation(agg_sb[:, :].rearrange("p (h k a) -> p k h a", h=2, k=Q),
                                   p_agg[1 - s][:, 0:2 * P].rearrange("p (k h a) -> p k h a", k=Q, h=2), ACT.Copy)\
                       .then_inc(agg_copied, 1)
                    act.wait_ge(xst_done, b + 1)
                    act.activation(xs_t[:, :], p_xst[:, 0:2 * P], ACT.Copy).then_inc(agg_copied, 1)

            def refill(g, s):
                act.wait_ge(cast_done, 8 * g + 8)
                load_adj(act, g + 2, s, (2, 3))

            for g in range(PEEL):
                step(g, g % 2)
                refill(g, g % 2)
            with act.Fori(PEEL, NB - 3, 2) as g0:
                for s in range(2):
                    step(g0 + s, s)
                    refill(g0 + s, s)
            for g in range(NB - 2, NB + 3):
                step(g, g % 2)
            act.wait_ge(exp_asked, 1)
            act.activation(route[:, 2, :], route[:, 0, :], ACT.Exp, bias=route[:, 1, 0:1],
                           accum_out=route[:, 3, 0:1]).then_inc(exp_done, 1)
            act.wait_ge(exp_asked, 2)
            act.activation(route[:, 10, :], route[:, 8, :], ACT.Exp, bias=route[:, 9, 0:1],
                           accum_out=route[:, 11, 0:1]).then_inc(exp_done, 1)
            act.wait_ge(exp_asked, 3)
            act.activation(route[:, 15, 0:TOPK], route[:, 13, 0:TOPK], ACT.Exp, bias=route[:, 14, 0:1],
                           accum_out=route[:, 16, 0:1]).then_inc(exp_done, 1)
            act.wait_ge(sel_done, 1)

            def gelus(f, s):
                for k in range(HC):
                    act.wait_ge(hid_mm_done, HC * f + k + 1)
                    if k == 0 and (not isinstance(f, int) or f >= 2):
                        act.wait_ge(y_mm_done, TC * f - TC)
                    act.activation(hid[s][k], bank[k][:, :], ACT.Gelu, bias=b1_sel[:, k // NC, k % NC:k % NC + 1])\
                       .then_inc(gelu_done, 1)
            gelus(0, 0)
            gelus(1, 1)
            with act.Fori(2, NF - 1, 2) as f0:
                gelus(f0, 0)
                gelus(f0 + 1, 1)

        @block.gpsimd
        def _(pool):
            for dst, src in (
                    (wg[:, :, :], gnn_weight.rearrange("(h f) o -> f h o", h=2)),
                    (bg_row[0:1, :], gnn_bias.unsqueeze(0)),
                    (wr[:, :], Wr),
                    (br_all[:, :], br.partition_broadcast(P)),
                    (gamma_all[:, :], gamma.partition_broadcast(P)),
                    (beta_all[:, :], beta.partition_broadcast(P)),
                    (w1_all[:, :].rearrange("d (e f) -> d e f", e=E), W1.rearrange("e d f -> d e f")),
                    (b1_rows[:, :], b1.rearrange("e (c f) -> (e c) f", c=NC))):
                pool.dma_start(dst, src).then_inc(weights_in, 16)
            pool.memset(ident[:, :], 0.0).then_inc(pool_step, 1)
            pool.memset(neg_half[:, :], -0.5).then_inc(pool_step, 1)
            pool.memset(eps_const[:, :], EPS).then_inc(eps_set, 1)
            pool.memset(split_const[:, :], SPLIT).then_inc(consts_done, 1)
            pool.wait_ge(pool_step, 2)
            pool.affine_select(out=ident[:, :], in_=ident[:, :], compare_op=ALU.not_equal, fill=1.0, base=0,
                               pattern=[[-1, P]], channel_multiplier=1).then_inc(consts_done, 1)
            pool.wait_ge(consts_done, 2)
            pool.tensor_tensor(lane_mask[:, :], ident[:, 0:L], ident[:, L:2 * L], ALU.add).then_inc(pool_step, 1)
            for q in range(2, Q):
                pool.wait_ge(pool_step, q + 1)
                pool.tensor_tensor(lane_mask[:, :], lane_mask[:, :], ident[:, q * L:q * L + L], ALU.add)\
                    .then_inc(pool_step, 1)
            pool.wait_ge(pool_step, 5)
            for g in range(4):
                r = rstd1[:, 8 * g:8 * g + 8]
                pool.wait_ge(stats1_done, 8 * (g + 1))
                pool.tensor_scalar(r, mv1[:, 8 * g:8 * g + 8, 1], EPS, None, ALU.add).then_inc(pool_step, 1)
                pool.wait_ge(pool_step, 5 + 3 * g + 1)
                pool.tensor_tensor(r, r, neg_half[:, 0:8], ALU.pow).then_inc(pool_step, 1)
                pool.wait_ge(pool_step, 5 + 3 * g + 2)
                pool.tensor_scalar(r, r, SPLIT, None, ALU.mult).then_inc(pool_step, 1)
                pool.wait_ge(pool_step, 5 + 3 * g + 3)
                pool.engine_nop().then_inc(rstd1_done, 1)

            def step(g, s):
                if live(g - 2):
                    b = g - 2
                    pool.wait_ge(stats2_done, 2 * b + 2)
                    pool.tensor_tensor(var2[:, :], mv2[s][:, :, 1], eps_const[:, 0:2], ALU.add).then_inc(var2_done, 1)
                    pool.wait_ge(var2_done, b + 1)
                    pool.tensor_tensor(rstd2[s][:, :], var2[:, :], neg_half[:, 0:2], ALU.pow)\
                        .then_inc(rstd2_done, 1)
                if live(g):
                    if not isinstance(g, int) or g >= 2:
                        pool.wait_ge(xst_done, g - 1)
                    pool.tensor_copy(xs_stage[s][:, :, :], xs[:, bass.ds(2 * g, 2), :]).then_inc(self_staged, 1)
                    pool.wait_ge(cast_done, 8 * g + 8)
                    if not isinstance(g, int) or g >= 2:
                        pool.wait_ge(proj_done, g - 1)
                    for h in range(2):
                        pool.tensor_tensor(
                            deg_spread[s][:, h, :, :, :],
                            lane_mask[:, 16 * h:16 * h + 16].unsqueeze(1).unsqueeze(3).broadcast_to([P, Q, 16, 2]),
                            deg_part[s][:, :, :].unsqueeze(2).broadcast_to([P, Q, 16, 2]), ALU.mult)\
                            .then_inc(spread_done, 1)
                if live(g - 2):
                    pool.wait_ge(norm2_done, 2 * b + 2)
                    pool.wait_ge(self_staged, b + 1)
                    pool.tensor_copy(xs[:, bass.ds(2 * b, 2), :], xn_stage[s][:, :, :]).then_inc(xn2_kept, 1)
                    pool.tensor_tensor(x_res[:, bass.ds(2 * b, 2), :], x2_stage[s][:, :, :], beta_all[:, :].unsqueeze(1).broadcast_to([P, 2, D]), ALU.add)\
                        .then_inc(beta_added, 1)

            pool.wait_ge(weights_in, 16 * 8)
            pool.wait_ge(eps_set, 1)
            pool.wait_ge(low_done, 4)
            for g in range(PEEL):
                step(g, g % 2)
            with pool.Fori(PEEL, NB - 1, 2) as g0:
                for s in range(2):
                    step(g0 + s, s)
            pool.wait_ge(cast_done, 8 * (NB - 1))
            pool.dma_start(w2_all, W2.rearrange("e (c f) d -> f (e c) d", c=NC)).then_inc(late_in, 16)
            pool.dma_start(b2_all, b2.rearrange("e d -> (e d)").partition_broadcast(P)).then_inc(late_in, 16)
            for g in range(NB, NB + 2):
                step(g, g % 2)

            def skips(f, s):
                pool.tensor_tensor(skip[s], xs[:, bass.ds(TC * f, TC), :],
                                   b2_sel[:, :].unsqueeze(1).broadcast_to([P, TC, D]), ALU.add)\
                    .then_inc(skip_done, 1)

            def rstds(f, s):
                pool.wait_ge(stats3_done, TC * (f + 1))
                pool.tensor_tensor(var3[s][:, :], mv3[s][:, :, 1], eps_const[:, :], ALU.add).then_inc(var3_done, 1)
                pool.wait_ge(var3_done, f + 1)
                pool.tensor_tensor(rstd3[s][:, :], var3[s][:, :], neg_half[:, 0:TC], ALU.pow)\
                    .then_inc(rstd3_done, 1)

            pool.wait_ge(sel_done, 1)
            pool.wait_ge(xn2_kept, NB)
            skips(0, 0)
            skips(1, 1)
            with pool.Fori(0, NF - 3, 2) as f0:
                for s in range(2):
                    rstds(f0 + s, s)
                    pool.wait_ge(ysum_done, f0 + s + 1)
                    skips(f0 + s + 2, s)
            rstds(NF - 2, 0)
            rstds(NF - 1, 1)

        @block.vector
        def _(dve):
            dve.wait_ge(x_in, 16 * Q)
            for b0 in range(0, T, 4):
                for b in range(b0, b0 + 4):
                    dve.bn_stats(bn6[:, b, :], x_res[:, b, :]).then_inc(bn1_done, 1)
                for b in range(b0, b0 + 4):
                    dve.wait_ge(bn1_done, b + 1)
                    dve.bn_aggr(mv1[:, b, :], bn6[:, b, :]).then_inc(stats1_done, 1)
            for g in range(4):
                dve.wait_ge(rstd1_done, g + 1)
                for b in range(8 * g, 8 * g + 8):
                    dve.tensor_scalar(xs[:, b, :], x_res[:, b, :], mv1[:, b, 0:1], rstd1[:, b:b + 1],
                                      ALU.subtract, ALU.mult).then_inc(norm1_done, 1)
            for g in range(4):
                dve.wait_ge(high_done, g + 1)
                dve.wait_ge(norm1_done, 8 * (g + 1))
                dve.tensor_tensor(xs_parts[:, 8 * g:8 * g + 8, 1, :], xs[:, 8 * g:8 * g + 8, :],
                                  xs_parts[:, 8 * g:8 * g + 8, 0, :], ALU.subtract).then_inc(low_done, 1)

            def turn(g, s, k):
                dve.wait_ge(cast_done, 8 * g + 2 * k + 2)
                dve.transpose(adj_t[s][:, k, :, :].rearrange("p b r -> p (b r)").bitcast(U32),
                              adj_pair[:, k, :, :].rearrange("p s e -> p (s e)").bitcast(U32)).then_inc(turned, 1)

            def residual_and_stats(b, s):
                dve.wait_ge(proj_done, b + 1)
                if not isinstance(b, int) or b >= 2:
                    dve.wait_ge(beta_added, b - 1)
                dve.scalar_tensor_tensor(x2_stage[s][:, :, :], p_self[:, 0:2 * P].rearrange("p (h d) -> p h d", h=2),
                                         1.0 / SPLIT, x_res[:, bass.ds(2 * b, 2), :], ALU.mult, ALU.add).then_inc(self_added, 1)
                dve.reciprocal(rdeg[:, :], p_deg[:, 0:2]).then_inc(self_added, 1)
                dve.wait_ge(self_added, 2 * b + 2)
                for h in range(2):
                    xh = x2_stage[s][:, h, :]
                    dve.scalar_tensor_tensor(xh, p_nb[:, h * P:h * P + P], rdeg[:, h:h + 1], xh,
                                             ALU.mult, ALU.add).then_inc(x2_done, 1)
                dve.wait_ge(x2_done, 2 * b + 2)
                for h in range(2):
                    dve.bn_stats(bn6b[:, h, :], x2_stage[s][:, h, :]).then_inc(bn2_done, 1)

            def aggregate_stats(s):
                for h in range(2):
                    dve.bn_aggr(mv2[s][:, h, :], bn6b[:, h, :]).then_inc(stats2_done, 1)

            def normalise(b, s):
                dve.wait_ge(rstd2_done, b + 1)
                dve.wait_ge(stats2_done, 2 * b + 2)
                if not isinstance(b, int) or b >= 2:
                    dve.wait_ge(xnt_done, b - 1)
                    dve.wait_ge(xn2_kept, b - 1)
                for h in range(2):
                    dve.tensor_scalar(xn_stage[s][:, h, :],
                                      x2_stage[s][:, h, :],
                                      mv2[s][:, h, 0:1], rstd2[s][:, h:h + 1],
                                      ALU.subtract, ALU.mult).then_inc(norm2_done, 1)

            def step(g, s):
                if live(g - 2):
                    residual_and_stats(g - 2, s)
                    dve.wait_ge(bn2_done, 2 * g - 2)
                if not live(g):
                    aggregate_stats(s)
                if live(g):
                    if not isinstance(g, int) or g >= 2:
                        dve.wait_ge(agg_done, g - 1)
                    turn(g, s, 0)
                    if live(g - 2):
                        aggregate_stats(s)
                    turn(g, s, 1)
                if live(g - 2):
                    normalise(g - 2, s)
                if live(g):
                    turn(g, s, 2)
                    turn(g, s, 3)

            for g in range(PEEL):
                step(g, g % 2)
            with dve.Fori(PEEL, NB - 1, 2) as g0:
                for s in range(2):
                    step(g0 + s, s)
            for g in range(NB, NB + 2):
                step(g, g % 2)

            links = [0]

            def link(ins):
                links[0] += 1
                ins.then_inc(chain, 1)
                dve.wait_ge(chain, links[0])

            def row(i, n=E):
                return route[:, i, 0:n]

            dve.wait_ge(weights_in, 16 * 8)
            dve.wait_ge(b1_turned, 1)
            link(dve.tensor_copy(b1_all[:, :], p_logit[:, P:P + E * NC]))
            dve.wait_ge(xnt_copied, NB)
            link(dve.reduce_sum(row(20, 1), col_sum[:, :], AX.X))
            dve.tensor_scalar(row(21), wr[:, :], row(20, 1), 1.0 / (N * SPLIT), ALU.mult, ALU.mult).then_inc(wr_scaled, 1)
            dve.wait_ge(logits_done, 1)
            link(dve.tensor_tensor(row(0), p_logit[:, 0:E], br_all[:, :], ALU.add))

            link(dve.reduce_max(row(17, 1), row(0), AX.X))
            dve.tensor_scalar(row(1, 1), row(17, 1), -1.0, None, ALU.mult).then_inc(exp_asked, 1)
            dve.wait_ge(exp_done, 1)
            link(dve.reciprocal(row(4, 1), row(3, 1)))
            link(dve.tensor_scalar(row(5), row(2), row(4, 1), None, ALU.mult))
            link(dve.tensor_scalar(row(6), row(5), float(N), None, ALU.mult))
            link(dve.reciprocal(row(7), row(6)))
            link(dve.tensor_scalar(row(18), row(7), CAPACITY, 1.0, ALU.mult, ALU.min))
            link(dve.tensor_tensor(row(8), row(5), row(18), ALU.mult))
            link(dve.reduce_max(row(17, 1), row(8), AX.X))
            dve.tensor_scalar(row(9, 1), row(17, 1), -1.0, None, ALU.mult).then_inc(exp_asked, 1)
            dve.wait_ge(exp_done, 2)
            link(dve.reciprocal(row(4, 1), row(11, 1)))
            link(dve.tensor_scalar(row(12), row(10), row(4, 1), None, ALU.mult))
            link(dve.max(row(13), row(12)))
            link(dve.max_index(top_idx[:, :], row(13), row(12)))
            dve.tensor_scalar(row(14, 1), row(13, 1), -1.0, None, ALU.mult).then_inc(exp_asked, 1)
            chosen = [dve.value_load(top_idx[0:1, k:k + 1], min_val=0, max_val=E - 1) for k in range(TOPK)]
            for k in range(TOPK):
                dve.tensor_copy(w1_sel[:, k * F:k * F + F], w1_all[:, bass.ds(chosen[k] * F, F)])
                dve.tensor_copy(b1_sel[:, k, :], b1_all[:, bass.ds(chosen[k] * NC, NC)])
            dve.wait_ge(exp_done, 3)
            dve.wait_ge(late_in, 32)
            link(dve.reciprocal(row(4, 1), row(16, 1)))
            link(dve.tensor_scalar(row(19, TOPK), row(15, TOPK), row(4, 1), None, ALU.mult))
            for k in range(TOPK):
                dve.tensor_scalar(w2_sel[:, NC * k:NC * k + NC, :], w2_all[:, bass.ds(chosen[k] * NC, NC), :],
                                  route[:, 19, k:k + 1], None, ALU.mult)
            link(dve.tensor_scalar(b2_sel[:, :], b2_all[:, bass.ds(chosen[0] * D, D)], route[:, 19, 0:1], None,
                                   ALU.mult))
            dve.scalar_tensor_tensor(b2_sel[:, :], b2_all[:, bass.ds(chosen[1] * D, D)], route[:, 19, 1:2],
                                     b2_sel[:, :], ALU.mult, ALU.add).then_inc(sel_done, 1)

            def add_up(f, s):
                dve.wait_ge(y_mm_done, TC * f + TC)
                dve.wait_ge(skip_done, f + 1)
                dve.tensor_tensor(ysum[s], bank[4 + s][:, :].rearrange("p (t d) -> p t d", t=TC), skip[s],
                                  ALU.add).then_inc(ysum_done, 1)
                dve.wait_ge(ysum_done, f + 1)
                for t in range(TC):
                    dve.bn_stats(bn6c[s][:, t, :], ysum[s][:, t, :]).then_inc(bn3_done, 1)

            def centre(f, s):
                for t in range(TC):
                    dve.bn_aggr(mv3[s][:, t, :], bn6c[s][:, t, :]).then_inc(stats3_done, 1)
                dve.wait_ge(stats3_done, TC * f + TC)
                for t in range(TC):
                    dve.scalar_tensor_tensor(centred[s][:, t, :], ysum[s][:, t, :], mv3[s][:, t, 0:1],
                                             gamma_all[:, :], ALU.subtract, ALU.mult).then_inc(centred_done, 1)

            def emit(f, s):
                dve.wait_ge(rstd3_done, f + 1)
                dve.wait_ge(centred_done, TC * f + TC)
                if not isinstance(f, int) or f >= 2:
                    dve.wait_ge(stored[s], 8 * Q * (f - s))
                for t in range(TC):
                    dve.scalar_tensor_tensor(result[s][:, t, :], centred[s][:, t, :], rstd3[s][:, t:t + 1],
                                             x_res[:, bass.ds(TC * f + t, 1), :].rearrange("p o d -> p (o d)"),
                                             ALU.mult, ALU.add).then_inc(result_done, 1)

            def pipelined(f, s):
                add_up(f, s)
                dve.wait_ge(bn3_done, TC * f + TC)
                emit(f - 1, 1 - s)
                centre(f, s)

            dve.wait_ge(beta_added, NB)
            add_up(0, 0)
            dve.wait_ge(bn3_done, TC)
            centre(0, 0)
            pipelined(1, 1)
            pipelined(2, 0)
            with dve.Fori(3, NF - 2, 2) as f0:
                pipelined(f0, 1)
                pipelined(f0 + 1, 0)
            pipelined(NF - 1, 1)
            emit(NF - 1, 1)

        @block.tensor
        def _(pe):
            pe.wait_ge(weights_in, 16 * 8)
            pe.wait_ge(consts_done, 2)
            pe.transpose(p_logit[:, P:P + E * NC], b1_rows[:, :], ident[0:E * NC, 0:E * NC]).then_inc(b1_turned, 1)

            def aggregate(g, s):
                pe.wait_ge(turned, 4 * g + 4)
                if not isinstance(g, int) or g >= 2:
                    pe.wait_ge(agg_copied, 2 * g - 2)
                for b in range(T):
                    if isinstance(g, int) and g == 0 and b % 8 == 0:
                        pe.wait_ge(low_done, b // 8 + 1)
                    for part in range(2):
                        mm = pe.matmul(p_agg[s][:, 0:2 * P].rearrange("p (k r) -> p k r", k=Q), xs_parts[:, b, part, :],
                                       adj_t[s][:, :, b, :], start=(b == 0 and part == 0),
                                       stop=(b == T - 1 and part == 1))
                mm.then_inc(agg_done, 1)
                if not isinstance(g, int) or g >= 1:
                    pe.wait_ge(agg_copied, 2 * g)
                pe.wait_ge(self_staged, g + 1)
                for h in range(2):
                    mm = pe.transpose(p_xst[:, h * P:h * P + P], xs_stage[s][:, h, :], ident[:, :])
                mm.then_inc(xst_done, 1)

            def project(b):
                pe.wait_ge(agg_copied, 2 * b + 2)
                if not isinstance(b, int) or b >= 1:
                    pe.wait_ge(x2_done, 2 * b)
                for h in range(2):
                    pe.matmul(p_nb[:, h * P:h * P + P], agg_sb[:, h * P:h * P + P], wg[:, 0, :], start=True, stop=True)
                for h in range(2):
                    pe.matmul(p_self[:, h * P:h * P + P], xs_t[:, h * P:h * P + P], wg[:, 1, :],
                              start=True, stop=False)
                    pe.matmul(p_self[:, h * P:h * P + P], split_const[0:1, :], bg_row[0:1, :],
                              start=False, stop=True)
                pe.wait_ge(spread_done, 2 * b + 2)

            def counts(b, s):
                for h in range(2):
                    mm = pe.matmul(p_deg[:, h:h + 1], deg_spread[s][:, h, :, :, :].rearrange("p k a e -> p (k a e)"),
                                   split_const[:, 0:1], start=True, stop=True)
                mm.then_inc(proj_done, 1)

            def turn_xn(b, s):
                pe.wait_ge(norm2_done, 2 * b + 2)
                if not isinstance(b, int) or b >= 1:
                    pe.wait_ge(xnt_copied, b)
                for h in range(2):
                    mm = pe.transpose(p_xnt[:, h * P:h * P + P], xn_stage[s][:, h, :], ident[:, :])
                mm.then_inc(xnt_done, 1)

            def step(g, s):
                if live(g):
                    aggregate(g, s)
                if live(g - 1):
                    project(g - 1)
                    counts(g - 1, 1 - s)
                if live(g - 2):
                    turn_xn(g - 2, s)

            for g in range(PEEL):
                step(g, g % 2)
            with pe.Fori(PEEL, NB - 1, 2) as g0:
                for s in range(2):
                    step(g0 + s, s)
            for g in range(NB, NB + 2):
                step(g, g % 2)

            pe.wait_ge(wr_scaled, 1)
            pe.matmul(p_logit[:, 0:E], split_const[:, :], route[:, 21, :], start=True, stop=True).then_inc(logits_done, 1)

            pe.wait_ge(sel_done, 1)

            def hidden(f):
                for k in range(HC):
                    if not isinstance(f, int) or f >= 1:
                        pe.wait_ge(gelu_done, HC * f - HC + k + 1)
                    pe.matmul(bank[k][:, :], w1_sel[:, k * P:k * P + P], xn_t[:, bass.ds(f * FW, FW)],
                              start=True, stop=True).then_inc(hid_mm_done, 1)

            def combine(f, s):
                if not isinstance(f, int) or f >= 2:
                    pe.wait_ge(ysum_done, f - 1)
                pe.wait_ge(gelu_done, HC * f + HC)
                for t in range(TC):
                    for k in range(HC):
                        mm = pe.matmul(bank[4 + s][:, t * P:t * P + P], hid[s][k][:, t * P:t * P + P],
                                       w2_sel[:, k, :], start=(k == 0), stop=(k == HC - 1))
                    mm.then_inc(y_mm_done, 1)

            hidden(0)
            hidden(1)
            combine(0, 0)
            hidden(2)
            combine(1, 1)
            hidden(3)
            combine(2, 0)
            with pe.Fori(3, NF - 2, 2) as f0:
                hidden(f0 + 1)
                combine(f0, 1)
                hidden(f0 + 2)
                combine(f0 + 1, 0)
            combine(NF - 1, 1)


_INS = ['x', 'adj', 'L0_gnn_weight', 'L0_gnn_bias', 'L0_ffn_Wr', 'L0_ffn_br', 'L0_ffn_W1', 'L0_ffn_b1',
        'L0_ffn_W2', 'L0_ffn_b2', 'L0_ffn_gamma', 'L0_ffn_beta']
_OUTS = [((4096, 128), 'float32')]


def kernel(**inputs):
    import numpy as _np
    import concourse.bacc as _bacc
    from concourse import mybir as _mybir
    from concourse.bass_utils import run_bass_kernel_spmd as _run

    nc = _bacc.Bacc("TRN2", target_bir_lowering=False, num_devices=1)
    arrays, args = {}, []
    for name in _INS:
        a = _np.ascontiguousarray(inputs[name])
        arrays[f"in_{name}_dram"] = a
        args.append(nc.dram_tensor(f"in_{name}_dram", a.shape, _mybir.dt.from_np(a.dtype), kind="ExternalInput").ap())
    for i, (shape, dtype) in enumerate(_OUTS):
        dt = _mybir.dt.from_np(_np.dtype(dtype))
        args.append(nc.dram_tensor(f"out_{i}_dram", shape, dt, kind="ExternalOutput").ap())
    gnn_moe_kernel(nc, *args)
    r = _run(nc, [arrays], core_ids=[0])
    return r.results[0]["out_0_dram"]
```

```python
import math
from contextlib import ExitStack

import concourse.bass as bass
from concourse import mybir
from concourse.alu_op_type import AluOpType as ALU

F32 = mybir.dt.float32
F32R = mybir.dt.float32r
F16 = mybir.dt.float16
I32 = mybir.dt.int32
U32 = mybir.dt.uint32
ACT = mybir.ActivationFunctionType
AX = mybir.AxisListType


def gnn_moe_kernel(nc, x, adj, gnn_weight, gnn_bias, Wr, br, W1, b1, W2, b2, gamma, beta, out):
    P = 128
    Q, L = 4, 32
    N, D = x.shape
    E, _, F = W1.shape
    T = N // P
    QS = N // Q
    NB = T // 2
    BR = QS // NB
    SPLIT = 4096.0
    EPS = 1e-5
    CAPACITY = float(math.ceil(N * 1.25 / E))
    TOPK = 2
    NC = F // P
    HC = TOPK * NC
    TC = 4
    NF = T // TC
    FW = TC * P
    PEEL = 5

    with ExitStack() as ctx:
        def sb(name, shape, dt=F32):
            return ctx.enter_context(nc.sbuf_tensor(name, shape, dt))

        def sem(name):
            return ctx.enter_context(nc.semaphore(name))

        adj_raw = [sb(f"adj_raw{s}", [P, Q, 2, QS], I32) for s in range(2)]
        adj_pair = sb("adj_pair", [P, Q, QS, 2], F16)
        adj_t = [sb(f"adj_t{s}", [P, Q, L, 2 * L], F16) for s in range(2)]
        deg_part = [sb(f"deg_part{s}", [P, Q, 2]) for s in range(2)]
        deg_spread = [sb(f"deg_spread{s}", [P, 2, Q, L // 2, 2]) for s in range(2)]
        xs_parts = sb("xs_parts", [P, T, 2, D], F16)
        x_res = sb("x_res", [P, T, D])
        xs = sb("xs", [P, T, D])
        xn_hi = sb("xn_hi", [P, T * P], F32R)
        xn_lo = sb("xn_lo", [P, T * P], F32R)
        w1_hi = sb("w1_hi", [P, TOPK * F], F32R)
        w1_lo = sb("w1_lo", [P, TOPK * F], F32R)
        b1_rows = sb("b1_rows", [E * NC, P])
        b1_all = sb("b1_all", [P, E * NC])
        wg = sb("wg", [P, 2, D])
        bg_row = sb("bg_row", [1, D])
        wr = sb("wr", [P, E])
        br_all = sb("br_all", [P, E])
        gamma_all = sb("gamma_all", [P, D])
        beta_all = sb("beta_all", [P, D])
        ident = sb("ident", [P, P])
        ident16 = sb("ident16", [P, P], F16)
        lane_mask = sb("lane_mask", [P, L])
        split_const = sb("split_const", [P, P])
        neg_half = sb("neg_half", [P, 8])
        eps_const = sb("eps_const", [P, TC])
        bn6 = sb("bn6", [P, T, 6])
        mv1 = sb("mv1", [P, T, 2])
        rstd1 = sb("rstd1", [P, T])
        bn6b = sb("bn6b", [P, 2, 6])
        x2_stage = [sb(f"x2_stage{s}", [P, 2, D]) for s in range(2)]
        xn_stage = [sb(f"xn_stage{s}", [P, 2, D]) for s in range(2)]
        mv2 = [sb(f"mv2_{s}", [P, 2, 2]) for s in range(2)]
        var2 = sb("var2", [P, 2])
        rstd2 = [sb(f"rstd2_{s}", [P, 2]) for s in range(2)]
        rdeg = sb("rdeg", [P, 2])
        agg_sb = sb("agg_sb", [P, 2 * P])
        xs_t = sb("xs_t", [P, 2 * P])
        col_sum = sb("col_sum", [P, NB])
        route = sb("route", [P, 24, E])
        top_idx = sb("top_idx", [P, 8], U32)
        b1_sel = sb("b1_sel", [P, TOPK, NC])
        b2_sel = sb("b2_sel", [P, D])
        free2 = adj_pair[:, :, :, :].rearrange("p k s e -> p (k s e)").bitcast(F32)
        w2_sel = free2[:, 0:HC * D].rearrange("p (k d) -> p k d", k=HC)
        free = adj_raw[0][:, :, :, :].rearrange("p k e s -> p (k e s)").bitcast(F32)
        free3 = adj_t[0][:, :, :, :].rearrange("p k b r -> p (k b r)").bitcast(F32)
        hid = [[free3[:, (s * HC + k) * FW:(s * HC + k + 1) * FW] for k in range(HC)] for s in range(2)]
        w1_all = free[:, 0:E * F]
        w2_all = free[:, E * F:E * F + E * NC * D].rearrange("p (k d) -> p k d", k=E * NC)
        b2_all = free[:, E * F + E * NC * D:E * F + E * NC * D + E * D]
        free1 = adj_raw[1][:, :, :, :].rearrange("p k e s -> p (k e s)").bitcast(F32)

        def slots(n):
            return [free1[:, (n + s) * FW:(n + s + 1) * FW].rearrange("p (t d) -> p t d", t=TC) for s in range(2)]
        skip, ysum, centred, result = slots(0), slots(2), slots(4), slots(6)
        bn6c = [sb(f"bn6c{s}", [P, TC, 6]) for s in range(2)]
        mv3 = [sb(f"mv3_{s}", [P, TC, 2]) for s in range(2)]
        var3 = [sb(f"var3_{s}", [P, TC]) for s in range(2)]
        rstd3 = [sb(f"rstd3_{s}", [P, TC]) for s in range(2)]

        bank = [ctx.enter_context(nc.psum_tensor(f"bank{i}", [P, 512], F32)) for i in range(8)]
        p_agg = [bank[0], bank[1]]
        p_xst, p_xnt, p_nb, p_self, p_deg = bank[2], bank[3], bank[4], bank[5], bank[6]
        p_logit = bank[7]

        x_in = sem("x_in")
        weights_in = sem("weights_in")
        eps_set = sem("eps_set")
        late_in = sem("late_in")
        xn2_kept = sem("xn2_kept")
        adj_in = [[sem(f"adj_in{s}_{e}") for e in range(2)] for s in range(2)]
        consts_done = sem("consts_done")
        pool_step = sem("pool_step")
        bn1_done = sem("bn1_done")
        stats1_done = sem("stats1_done")
        rstd1_done = sem("rstd1_done")
        norm1_done = sem("norm1_done")
        high_done = sem("high_done")
        low_done = sem("low_done")
        cast_done = sem("cast_done")
        turned = sem("turned")
        spread_done = sem("spread_done")
        agg_done = sem("agg_done")
        xst_done = sem("xst_done")
        agg_copied = sem("agg_copied")
        proj_done = sem("proj_done")
        self_added = sem("self_added")
        x2_done = sem("x2_done")
        bn2_done = sem("bn2_done")
        stats2_done = sem("stats2_done")
        var2_done = sem("var2_done")
        rstd2_done = sem("rstd2_done")
        norm2_done = sem("norm2_done")
        xnt_done = sem("xnt_done")
        xnt_copied = sem("xnt_copied")
        xn_lo_done = sem("xn_lo_done")
        w1_ready = sem("w1_ready")
        beta_added = sem("beta_added")
        chain = sem("chain")
        wr_scaled = sem("wr_scaled")
        b1_turned = sem("b1_turned")
        logits_done = sem("logits_done")
        exp_asked = sem("exp_asked")
        exp_done = sem("exp_done")
        sel_done = sem("sel_done")
        hid_mm_done = sem("hid_mm_done")
        gelu_done = sem("gelu_done")
        y_mm_done = sem("y_mm_done")
        skip_done = sem("skip_done")
        ysum_done = sem("ysum_done")
        bn3_done = sem("bn3_done")
        stats3_done = sem("stats3_done")
        var3_done = sem("var3_done")
        rstd3_done = sem("rstd3_done")
        centred_done = sem("centred_done")
        result_done = sem("result_done")
        stored = [sem(f"stored{s}") for s in range(2)]

        x_q = x.rearrange("(q b a) f -> q a b f", q=Q, b=T, a=L)
        out_q = out.rearrange("(q b a) f -> q a b f", q=Q, b=T, a=L)
        adj_v = adj.rearrange("(k n c e) (q s) -> n e q c k s", k=Q, n=NB, c=L, e=2, q=Q)

        block = ctx.enter_context(nc.Block())

        def live(b):
            return not isinstance(b, int) or 0 <= b < NB

        def load_adj(eng, b, s, e, q):
            eng.dma_start(adj_raw[s][32 * q:32 * q + 32, :, e, :], adj_v[b, e, q]).then_inc(adj_in[s][e], 16)

        @block.sync
        def _(sp):
            for q in range(2):
                sp.dma_start(x_res[32 * q:32 * q + 32, :, :], x_q[q]).then_inc(x_in, 16)
            for s in range(2):
                for e in range(2):
                    for q in range(2):
                        load_adj(sp, s, s, e, q)
            with sp.Fori(2, NB - 1, 2) as b0:
                for s in range(2):
                    b = b0 + s
                    for e in range(2):
                        sp.wait_ge(cast_done, 8 * b - 12 + 4 * e)
                        for q in range(2):
                            load_adj(sp, b, s, e, q)
            for f in range(NF):
                sp.wait_ge(result_done, TC * (f + 1))
                for q in range(Q):
                    sp.dma_start(out_q[q][:, TC * f:TC * f + TC, :], result[f % 2][32 * q:32 * q + 32, :, :])\
                      .then_inc(stored[f % 2], 16)
            for s in range(2):
                sp.wait_ge(stored[s], 16 * Q * NF // 2)

        @block.scalar
        def _(act):
            for q in range(2, Q):
                act.dma_start(x_res[32 * q:32 * q + 32, :, :], x_q[q]).then_inc(x_in, 16)
            for s in range(2):
                for e in range(2):
                    for q in range(2, Q):
                        load_adj(act, s, s, e, q)
            for g in range(4):
                act.wait_ge(norm1_done, 8 * (g + 1))
                act.activation(xs_parts[:, 8 * g:8 * g + 8, 0, :], xs[:, 8 * g:8 * g + 8, :], ACT.Copy)\
                   .then_inc(high_done, 1)

            def refill(g, s, e, q):
                if e == 0 and live(g + 1) and (not isinstance(g, int) or g >= 1):
                    act.wait_ge(cast_done, 8 * g)
                    load_adj(act, g + 1, 1 - s, 1, q)
                if e == 1 and live(g + 2):
                    act.wait_ge(cast_done, 8 * g + 4)
                    load_adj(act, g + 2, s, 0, q)

            def step(g, s):
                if live(g):
                    if not isinstance(g, int) or g >= 2:
                        act.wait_ge(spread_done, 2 * g - 2)
                    for e in range(2):
                        act.wait_ge(adj_in[s][e], 32 * (g - s) + 64)
                        for k in range(Q):
                            if e == 0 and (not isinstance(g, int) or g >= 1):
                                act.wait_ge(turned, 4 * g - 3 + k)
                            act.activation(adj_pair[:, k, :, e], adj_raw[s][:, k, e, :], ACT.Copy,
                                           accum_out=deg_part[s][:, k, e:e + 1]).then_inc(cast_done, 1)
                            if k < 2:
                                refill(g, s, e, 2 + k)
                if live(g - 4):
                    b = g - 4
                    act.wait_ge(xnt_done, b + 1)
                    act.activation(xn_hi[:, bass.ds(b * 2 * P, 2 * P)], p_xnt[:, 0:2 * P], ACT.Copy,
                                   accum_out=col_sum[:, bass.ds(b, 1)]).then_inc(xnt_copied, 1)
                if live(g - 1):
                    b = g - 1
                    if not isinstance(b, int) or b >= 1:
                        act.wait_ge(proj_done, b)
                    act.wait_ge(agg_done, b + 1)
                    act.activation(agg_sb[:, :].rearrange("p (h k a) -> p k h a", h=2, k=Q),
                                   p_agg[1 - s][:, 0:2 * P].rearrange("p (k h a) -> p k h a", k=Q, h=2), ACT.Copy)\
                       .then_inc(agg_copied, 1)
                    act.wait_ge(xst_done, b + 1)
                    act.activation(xs_t[:, :], p_xst[:, 0:2 * P], ACT.Copy).then_inc(agg_copied, 1)

            for g in range(PEEL):
                step(g, g % 2)
            with act.Fori(PEEL, NB - 4, 2) as g0:
                for j in range(2):
                    step(g0 + j, (PEEL + j) % 2)
            for g in range(NB - 3, NB + 4):
                step(g, g % 2)
            act.wait_ge(exp_asked, 1)
            act.activation(route[:, 2, :], route[:, 0, :], ACT.Exp, bias=route[:, 1, 0:1],
                           accum_out=route[:, 3, 0:1]).then_inc(exp_done, 1)
            act.wait_ge(exp_asked, 2)
            act.activation(route[:, 10, :], route[:, 8, :], ACT.Exp, bias=route[:, 9, 0:1],
                           accum_out=route[:, 11, 0:1]).then_inc(exp_done, 1)
            act.wait_ge(exp_asked, 3)
            act.activation(route[:, 15, 0:TOPK], route[:, 13, 0:TOPK], ACT.Exp, bias=route[:, 14, 0:1],
                           accum_out=route[:, 16, 0:1]).then_inc(exp_done, 1)
            act.wait_ge(sel_done, 1)

            def gelus(f, s):
                for k in range(HC):
                    act.wait_ge(hid_mm_done, HC * f + k + 1)
                    if k == 0 and (not isinstance(f, int) or f >= 2):
                        act.wait_ge(y_mm_done, TC * f - TC)
                    act.activation(hid[s][k], bank[k][:, :], ACT.Gelu, bias=b1_sel[:, k // NC, k % NC:k % NC + 1])\
                       .then_inc(gelu_done, 1)
            gelus(0, 0)
            gelus(1, 1)
            with act.Fori(2, NF - 1, 2) as f0:
                gelus(f0, 0)
                gelus(f0 + 1, 1)

        @block.gpsimd
        def _(pool):
            for dst, src in (
                    (wg[:, :, :], gnn_weight.rearrange("(h f) o -> f h o", h=2)),
                    (bg_row[0:1, :], gnn_bias.unsqueeze(0)),
                    (wr[:, :], Wr),
                    (br_all[:, :], br.partition_broadcast(P)),
                    (gamma_all[:, :], gamma.partition_broadcast(P)),
                    (beta_all[:, :], beta.partition_broadcast(P)),
                    (b1_rows[:, :], b1.rearrange("e (c f) -> (e c) f", c=NC))):
                pool.dma_start(dst, src).then_inc(weights_in, 16)
            pool.memset(ident[:, :], 0.0).then_inc(pool_step, 1)
            pool.memset(neg_half[:, :], -0.5).then_inc(pool_step, 1)
            pool.memset(eps_const[:, :], EPS).then_inc(eps_set, 1)
            pool.memset(split_const[:, :], SPLIT).then_inc(consts_done, 1)
            pool.wait_ge(pool_step, 2)
            pool.affine_select(out=ident[:, :], in_=ident[:, :], compare_op=ALU.not_equal, fill=1.0, base=0,
                               pattern=[[-1, P]], channel_multiplier=1).then_inc(consts_done, 1)
            pool.wait_ge(consts_done, 2)
            pool.tensor_copy(ident16[:, :], ident[:, :]).then_inc(consts_done, 1)
            pool.tensor_tensor(lane_mask[:, :], ident[:, 0:L], ident[:, L:2 * L], ALU.add).then_inc(pool_step, 1)
            for q in range(2, Q):
                pool.wait_ge(pool_step, q + 1)
                pool.tensor_tensor(lane_mask[:, :], lane_mask[:, :], ident[:, q * L:q * L + L], ALU.add)\
                    .then_inc(pool_step, 1)
            pool.wait_ge(pool_step, 5)
            for g in range(4):
                r = rstd1[:, 8 * g:8 * g + 8]
                pool.wait_ge(stats1_done, 8 * (g + 1))
                pool.tensor_scalar(r, mv1[:, 8 * g:8 * g + 8, 1], EPS, None, ALU.add).then_inc(pool_step, 1)
                pool.wait_ge(pool_step, 5 + 3 * g + 1)
                pool.tensor_tensor(r, r, neg_half[:, 0:8], ALU.pow).then_inc(pool_step, 1)
                pool.wait_ge(pool_step, 5 + 3 * g + 2)
                pool.tensor_scalar(r, r, SPLIT, None, ALU.mult).then_inc(pool_step, 1)
                pool.wait_ge(pool_step, 5 + 3 * g + 3)
                pool.engine_nop().then_inc(rstd1_done, 1)

            def step(g, s):
                if live(g - 3):
                    b = g - 3
                    pool.wait_ge(stats2_done, 2 * b + 2)
                    pool.tensor_tensor(var2[:, :], mv2[1 - s][:, :, 1], eps_const[:, 0:2], ALU.add).then_inc(var2_done, 1)
                    pool.wait_ge(var2_done, b + 1)
                    pool.tensor_tensor(rstd2[1 - s][:, :], var2[:, :], neg_half[:, 0:2], ALU.pow)\
                        .then_inc(rstd2_done, 1)
                if live(g):
                    pool.wait_ge(cast_done, 8 * g + 8)
                    if not isinstance(g, int) or g >= 2:
                        pool.wait_ge(proj_done, g - 1)
                    for h in range(2):
                        pool.tensor_tensor(
                            deg_spread[s][:, h, :, :, :],
                            lane_mask[:, 16 * h:16 * h + 16].unsqueeze(1).unsqueeze(3).broadcast_to([P, Q, 16, 2]),
                            deg_part[s][:, :, :].unsqueeze(2).broadcast_to([P, Q, 16, 2]), ALU.mult)\
                            .then_inc(spread_done, 1)
                if live(g - 3):
                    pool.wait_ge(norm2_done, 2 * b + 2)
                    pool.tensor_copy(xs[:, bass.ds(2 * b, 2), :], xn_stage[1 - s][:, :, :]).then_inc(xn2_kept, 1)
                    pool.tensor_tensor(x_res[:, bass.ds(2 * b, 2), :], x2_stage[1 - s][:, :, :], beta_all[:, :].unsqueeze(1).broadcast_to([P, 2, D]), ALU.add)\
                        .then_inc(beta_added, 1)

            pool.wait_ge(weights_in, 16 * 7)
            pool.wait_ge(eps_set, 1)
            pool.wait_ge(low_done, 4)
            for g in range(PEEL):
                step(g, g % 2)
            with pool.Fori(PEEL, NB - 2, 2) as g0:
                for j in range(2):
                    step(g0 + j, (PEEL + j) % 2)
            step(NB - 1, 1)
            pool.wait_ge(cast_done, 8 * (NB - 1))
            pool.dma_start(w1_all.rearrange("d (e f) -> d e f", e=E), W1.rearrange("e d f -> d e f"))\
                .then_inc(late_in, 16)
            pool.dma_start(w2_all, W2.rearrange("e (c f) d -> f (e c) d", c=NC)).then_inc(late_in, 16)
            pool.dma_start(b2_all, b2.rearrange("e d -> (e d)").partition_broadcast(P)).then_inc(late_in, 16)
            for g in range(NB, NB + 3):
                step(g, g % 2)

            def skips(f, s):
                pool.tensor_tensor(skip[s], xs[:, bass.ds(TC * f, TC), :],
                                   b2_sel[:, :].unsqueeze(1).broadcast_to([P, TC, D]), ALU.add)\
                    .then_inc(skip_done, 1)

            def rstds(f, s):
                pool.wait_ge(stats3_done, TC * (f + 1))
                pool.tensor_tensor(var3[s][:, :], mv3[s][:, :, 1], eps_const[:, :], ALU.add).then_inc(var3_done, 1)
                pool.wait_ge(var3_done, f + 1)
                pool.tensor_tensor(rstd3[s][:, :], var3[s][:, :], neg_half[:, 0:TC], ALU.pow)\
                    .then_inc(rstd3_done, 1)

            pool.wait_ge(sel_done, 1)
            pool.wait_ge(xn2_kept, NB)
            skips(0, 0)
            skips(1, 1)
            with pool.Fori(0, NF - 3, 2) as f0:
                for s in range(2):
                    rstds(f0 + s, s)
                    pool.wait_ge(ysum_done, f0 + s + 1)
                    skips(f0 + s + 2, s)
            rstds(NF - 2, 0)
            rstds(NF - 1, 1)

        @block.vector
        def _(dve):
            dve.wait_ge(x_in, 16 * Q)
            for b0 in range(0, T, 4):
                for b in range(b0, b0 + 4):
                    dve.bn_stats(bn6[:, b, :], x_res[:, b, :]).then_inc(bn1_done, 1)
                for b in range(b0, b0 + 4):
                    dve.wait_ge(bn1_done, b + 1)
                    dve.bn_aggr(mv1[:, b, :], bn6[:, b, :]).then_inc(stats1_done, 1)
            for g in range(4):
                dve.wait_ge(rstd1_done, g + 1)
                for b in range(8 * g, 8 * g + 8):
                    dve.tensor_scalar(xs[:, b, :], x_res[:, b, :], mv1[:, b, 0:1], rstd1[:, b:b + 1],
                                      ALU.subtract, ALU.mult).then_inc(norm1_done, 1)
            for g in range(4):
                dve.wait_ge(high_done, g + 1)
                dve.wait_ge(norm1_done, 8 * (g + 1))
                dve.tensor_tensor(xs_parts[:, 8 * g:8 * g + 8, 1, :], xs[:, 8 * g:8 * g + 8, :],
                                  xs_parts[:, 8 * g:8 * g + 8, 0, :], ALU.subtract).then_inc(low_done, 1)

            def turn(g, s, k):
                dve.wait_ge(cast_done, 8 * g + 5 + k)
                dve.transpose(adj_t[s][:, k, :, :].rearrange("p b r -> p (b r)").bitcast(U32),
                              adj_pair[:, k, :, :].rearrange("p s e -> p (s e)").bitcast(U32)).then_inc(turned, 1)

            def residual_and_stats(b, s):
                dve.wait_ge(proj_done, b + 1)
                if not isinstance(b, int) or b >= 2:
                    dve.wait_ge(beta_added, b - 1)
                dve.scalar_tensor_tensor(x2_stage[s][:, :, :], p_self[:, 0:2 * P].rearrange("p (h d) -> p h d", h=2),
                                         1.0 / SPLIT, x_res[:, bass.ds(2 * b, 2), :], ALU.mult, ALU.add).then_inc(self_added, 1)
                dve.reciprocal(rdeg[:, :], p_deg[:, 0:2]).then_inc(self_added, 1)
                dve.wait_ge(self_added, 2 * b + 2)
                for h in range(2):
                    xh = x2_stage[s][:, h, :]
                    dve.scalar_tensor_tensor(xh, p_nb[:, h * P:h * P + P], rdeg[:, h:h + 1], xh,
                                             ALU.mult, ALU.add).then_inc(x2_done, 1)
                dve.wait_ge(x2_done, 2 * b + 2)
                for h in range(2):
                    dve.bn_stats(bn6b[:, h, :], x2_stage[s][:, h, :]).then_inc(bn2_done, 1)

            def aggregate_stats(s):
                for h in range(2):
                    dve.bn_aggr(mv2[s][:, h, :], bn6b[:, h, :]).then_inc(stats2_done, 1)

            def normalise(b, s):
                dve.wait_ge(rstd2_done, b + 1)
                dve.wait_ge(stats2_done, 2 * b + 2)
                if not isinstance(b, int) or b >= 2:
                    dve.wait_ge(xnt_done, b - 1)
                    dve.wait_ge(xn2_kept, b - 1)
                for h in range(2):
                    dve.tensor_scalar(xn_stage[s][:, h, :],
                                      x2_stage[s][:, h, :],
                                      mv2[s][:, h, 0:1], rstd2[s][:, h:h + 1],
                                      ALU.subtract, ALU.mult).then_inc(norm2_done, 1)

            def low_part(b):
                dve.wait_ge(xnt_copied, b + 1)
                cols = bass.ds(b * 2 * P, 2 * P)
                dve.tensor_tensor(xn_lo[:, cols], p_xnt[:, 0:2 * P], xn_hi[:, cols].bitcast(F32), ALU.subtract)\
                   .then_inc(xn_lo_done, 1)

            def step(g, s):
                if live(g - 3):
                    dve.wait_ge(bn2_done, 2 * g - 4)
                if live(g):
                    if not isinstance(g, int) or g >= 2:
                        dve.wait_ge(agg_done, g - 1)
                    turn(g, s, 0)
                if live(g - 3):
                    aggregate_stats(1 - s)
                if live(g):
                    turn(g, s, 1)
                    turn(g, s, 2)
                if live(g - 3):
                    normalise(g - 3, 1 - s)
                if live(g):
                    turn(g, s, 3)
                if live(g - 2):
                    residual_and_stats(g - 2, s)
                if live(g - 4):
                    low_part(g - 4)

            for g in range(PEEL):
                step(g, g % 2)
            with dve.Fori(PEEL, NB - 2, 2) as g0:
                for j in range(2):
                    step(g0 + j, (PEEL + j) % 2)
            for g in range(NB - 1, NB + 4):
                step(g, g % 2)

            links = [0]

            def link(ins):
                links[0] += 1
                ins.then_inc(chain, 1)
                dve.wait_ge(chain, links[0])

            def row(i, n=E):
                return route[:, i, 0:n]

            dve.wait_ge(weights_in, 16 * 7)
            dve.wait_ge(b1_turned, 1)
            link(dve.tensor_copy(b1_all[:, :], p_logit[:, P:P + E * NC]))
            dve.wait_ge(xnt_copied, NB)
            link(dve.reduce_sum(row(20, 1), col_sum[:, :], AX.X))
            dve.tensor_scalar(row(21), wr[:, :], row(20, 1), 1.0 / (N * SPLIT), ALU.mult, ALU.mult).then_inc(wr_scaled, 1)
            dve.wait_ge(logits_done, 1)
            link(dve.tensor_tensor(row(0), p_logit[:, 0:E], br_all[:, :], ALU.add))

            link(dve.reduce_max(row(17, 1), row(0), AX.X))
            dve.tensor_scalar(row(1, 1), row(17, 1), -1.0, None, ALU.mult).then_inc(exp_asked, 1)
            dve.wait_ge(exp_done, 1)
            link(dve.reciprocal(row(4, 1), row(3, 1)))
            link(dve.tensor_scalar(row(5), row(2), row(4, 1), None, ALU.mult))
            link(dve.tensor_scalar(row(6), row(5), float(N), None, ALU.mult))
            link(dve.reciprocal(row(7), row(6)))
            link(dve.tensor_scalar(row(18), row(7), CAPACITY, 1.0, ALU.mult, ALU.min))
            link(dve.tensor_tensor(row(8), row(5), row(18), ALU.mult))
            link(dve.reduce_max(row(17, 1), row(8), AX.X))
            dve.tensor_scalar(row(9, 1), row(17, 1), -1.0, None, ALU.mult).then_inc(exp_asked, 1)
            dve.wait_ge(exp_done, 2)
            link(dve.reciprocal(row(4, 1), row(11, 1)))
            link(dve.tensor_scalar(row(12), row(10), row(4, 1), None, ALU.mult))
            link(dve.max(row(13), row(12)))
            link(dve.max_index(top_idx[:, :], row(13), row(12)))
            dve.tensor_scalar(row(14, 1), row(13, 1), -1.0, None, ALU.mult).then_inc(exp_asked, 1)
            chosen = [dve.value_load(top_idx[0:1, k:k + 1], min_val=0, max_val=E - 1) for k in range(TOPK)]
            dve.wait_ge(late_in, 48)
            for k in range(TOPK):
                dve.tensor_copy(w1_hi[:, k * F:k * F + F], w1_all[:, bass.ds(chosen[k] * F, F)]).then_inc(w1_ready, 1)
            for k in range(TOPK):
                dve.wait_ge(w1_ready, k + 1)
                dve.tensor_tensor(w1_lo[:, k * F:k * F + F], w1_all[:, bass.ds(chosen[k] * F, F)],
                                  w1_hi[:, k * F:k * F + F].bitcast(F32), ALU.subtract).then_inc(w1_ready, 1)
            for k in range(TOPK):
                dve.tensor_copy(b1_sel[:, k, :], b1_all[:, bass.ds(chosen[k] * NC, NC)])
            dve.wait_ge(exp_done, 3)
            link(dve.reciprocal(row(4, 1), row(16, 1)))
            link(dve.tensor_scalar(row(19, TOPK), row(15, TOPK), row(4, 1), None, ALU.mult))
            for k in range(TOPK):
                dve.tensor_scalar(w2_sel[:, NC * k:NC * k + NC, :], w2_all[:, bass.ds(chosen[k] * NC, NC), :],
                                  route[:, 19, k:k + 1], None, ALU.mult)
            link(dve.tensor_scalar(b2_sel[:, :], b2_all[:, bass.ds(chosen[0] * D, D)], route[:, 19, 0:1], None,
                                   ALU.mult))
            dve.scalar_tensor_tensor(b2_sel[:, :], b2_all[:, bass.ds(chosen[1] * D, D)], route[:, 19, 1:2],
                                     b2_sel[:, :], ALU.mult, ALU.add).then_inc(sel_done, 1)

            def add_up(f, s):
                dve.wait_ge(y_mm_done, TC * f + TC)
                dve.wait_ge(skip_done, f + 1)
                dve.tensor_tensor(ysum[s], bank[4 + s][:, :].rearrange("p (t d) -> p t d", t=TC), skip[s],
                                  ALU.add).then_inc(ysum_done, 1)
                dve.wait_ge(ysum_done, f + 1)
                for t in range(TC):
                    dve.bn_stats(bn6c[s][:, t, :], ysum[s][:, t, :]).then_inc(bn3_done, 1)

            def centre(f, s):
                for t in range(TC):
                    dve.bn_aggr(mv3[s][:, t, :], bn6c[s][:, t, :]).then_inc(stats3_done, 1)
                dve.wait_ge(stats3_done, TC * f + TC)
                for t in range(TC):
                    dve.scalar_tensor_tensor(centred[s][:, t, :], ysum[s][:, t, :], mv3[s][:, t, 0:1],
                                             gamma_all[:, :], ALU.subtract, ALU.mult).then_inc(centred_done, 1)

            def emit(f, s):
                dve.wait_ge(rstd3_done, f + 1)
                dve.wait_ge(centred_done, TC * f + TC)
                if not isinstance(f, int) or f >= 2:
                    dve.wait_ge(stored[s], 8 * Q * (f - s))
                for t in range(TC):
                    dve.scalar_tensor_tensor(result[s][:, t, :], centred[s][:, t, :], rstd3[s][:, t:t + 1],
                                             x_res[:, bass.ds(TC * f + t, 1), :].rearrange("p o d -> p (o d)"),
                                             ALU.mult, ALU.add).then_inc(result_done, 1)

            def pipelined(f, s):
                add_up(f, s)
                dve.wait_ge(bn3_done, TC * f + TC)
                emit(f - 1, 1 - s)
                centre(f, s)

            dve.wait_ge(beta_added, NB)
            add_up(0, 0)
            dve.wait_ge(bn3_done, TC)
            centre(0, 0)
            pipelined(1, 1)
            pipelined(2, 0)
            with dve.Fori(3, NF - 2, 2) as f0:
                pipelined(f0, 1)
                pipelined(f0 + 1, 0)
            pipelined(NF - 1, 1)
            emit(NF - 1, 1)

        @block.tensor
        def _(pe):
            pe.wait_ge(weights_in, 16 * 7)
            pe.wait_ge(consts_done, 3)
            pe.transpose(p_logit[:, P:P + E * NC], b1_rows[:, :], ident[0:E * NC, 0:E * NC]).then_inc(b1_turned, 1)

            def aggregate(g, s):
                pe.wait_ge(turned, 4 * g + 4)
                if not isinstance(g, int) or g >= 2:
                    pe.wait_ge(agg_copied, 2 * g - 2)
                for b in range(T):
                    if isinstance(g, int) and g == 0 and b % 8 == 0:
                        pe.wait_ge(low_done, b // 8 + 1)
                    for part in range(2):
                        mm = pe.matmul(p_agg[s][:, 0:2 * P].rearrange("p (k r) -> p k r", k=Q), xs_parts[:, b, part, :],
                                       adj_t[s][:, :, b, :], start=(b == 0 and part == 0),
                                       stop=(b == T - 1 and part == 1))
                mm.then_inc(agg_done, 1)
                if not isinstance(g, int) or g >= 1:
                    pe.wait_ge(agg_copied, 2 * g)
                for h in range(2):
                    for part in range(2):
                        mm = pe.matmul(p_xst[:, h * P:h * P + P],
                                       xs_parts[:, bass.ds(2 * g + h, 1), part, :].rearrange("p o d -> p (o d)"),
                                       ident16[:, :], start=(part == 0), stop=(part == 1))
                mm.then_inc(xst_done, 1)

            def project(b):
                pe.wait_ge(agg_copied, 2 * b + 2)
                if not isinstance(b, int) or b >= 1:
                    pe.wait_ge(x2_done, 2 * b)
                for h in range(2):
                    pe.matmul(p_nb[:, h * P:h * P + P], agg_sb[:, h * P:h * P + P], wg[:, 0, :], start=True, stop=True)
                for h in range(2):
                    pe.matmul(p_self[:, h * P:h * P + P], xs_t[:, h * P:h * P + P], wg[:, 1, :],
                              start=True, stop=False)
                    pe.matmul(p_self[:, h * P:h * P + P], split_const[0:1, :], bg_row[0:1, :],
                              start=False, stop=True)
                pe.wait_ge(spread_done, 2 * b + 2)

            def counts(b, s):
                for h in range(2):
                    mm = pe.matmul(p_deg[:, h:h + 1], deg_spread[s][:, h, :, :, :].rearrange("p k a e -> p (k a e)"),
                                   split_const[:, 0:1], start=True, stop=True)
                mm.then_inc(proj_done, 1)

            def turn_xn(b, s):
                pe.wait_ge(norm2_done, 2 * b + 2)
                if not isinstance(b, int) or b >= 1:
                    pe.wait_ge(xn_lo_done, b)
                for h in range(2):
                    mm = pe.transpose(p_xnt[:, h * P:h * P + P], xn_stage[s][:, h, :], ident[:, :])
                mm.then_inc(xnt_done, 1)

            def step(g, s):
                if live(g):
                    aggregate(g, s)
                if live(g - 1):
                    project(g - 1)
                    counts(g - 1, 1 - s)
                if live(g - 3):
                    turn_xn(g - 3, 1 - s)

            for g in range(PEEL):
                step(g, g % 2)
            with pe.Fori(PEEL, NB - 2, 2) as g0:
                for j in range(2):
                    step(g0 + j, (PEEL + j) % 2)
            for g in range(NB - 1, NB + 3):
                step(g, g % 2)

            pe.wait_ge(wr_scaled, 1)
            pe.matmul(p_logit[:, 0:E], split_const[:, :], route[:, 21, :], start=True, stop=True).then_inc(logits_done, 1)

            pe.wait_ge(w1_ready, 2 * TOPK)
            pe.wait_ge(xn_lo_done, NB)

            def hidden(f):
                for k in range(HC):
                    if not isinstance(f, int) or f >= 1:
                        pe.wait_ge(gelu_done, HC * f - HC + k + 1)
                    ks, cols = slice(k * P, k * P + P), bass.ds(f * FW, FW)
                    pe.matmul(bank[k][:, :], w1_hi[:, ks], xn_hi[:, cols], start=True, stop=False)
                    pe.matmul(bank[k][:, :], w1_hi[:, ks], xn_lo[:, cols], start=False, stop=False)
                    pe.matmul(bank[k][:, :], w1_lo[:, ks], xn_hi[:, cols], start=False, stop=True)\
                        .then_inc(hid_mm_done, 1)

            def combine(f, s):
                if not isinstance(f, int) or f >= 2:
                    pe.wait_ge(ysum_done, f - 1)
                pe.wait_ge(gelu_done, HC * f + HC)
                for t in range(TC):
                    for k in range(HC):
                        mm = pe.matmul(bank[4 + s][:, t * P:t * P + P], hid[s][k][:, t * P:t * P + P],
                                       w2_sel[:, k, :], start=(k == 0), stop=(k == HC - 1))
                    mm.then_inc(y_mm_done, 1)

            hidden(0)
            hidden(1)
            pe.wait_ge(sel_done, 1)
            combine(0, 0)
            hidden(2)
            combine(1, 1)
            hidden(3)
            combine(2, 0)
            with pe.Fori(3, NF - 2, 2) as f0:
                hidden(f0 + 1)
                combine(f0, 1)
                hidden(f0 + 2)
                combine(f0 + 1, 0)
            combine(NF - 1, 1)


_INS = ['x', 'adj', 'L0_gnn_weight', 'L0_gnn_bias', 'L0_ffn_Wr', 'L0_ffn_br', 'L0_ffn_W1', 'L0_ffn_b1',
        'L0_ffn_W2', 'L0_ffn_b2', 'L0_ffn_gamma', 'L0_ffn_beta']
_OUTS = [((4096, 128), 'float32')]


def kernel(**inputs):
    import numpy as _np
    import concourse.bacc as _bacc
    from concourse import mybir as _mybir
    from concourse.bass_utils import run_bass_kernel_spmd as _run

    nc = _bacc.Bacc("TRN2", target_bir_lowering=False, num_devices=1, dynamic_dma_scratch_size=8192)
    arrays, args = {}, []
    for name in _INS:
        a = _np.ascontiguousarray(inputs[name])
        arrays[f"in_{name}_dram"] = a
        args.append(nc.dram_tensor(f"in_{name}_dram", a.shape, _mybir.dt.from_np(a.dtype), kind="ExternalInput").ap())
    for i, (shape, dtype) in enumerate(_OUTS):
        dt = _mybir.dt.from_np(_np.dtype(dtype))
        args.append(nc.dram_tensor(f"out_{i}_dram", shape, dt, kind="ExternalOutput").ap())
    gnn_moe_kernel(nc, *args)
    r = _run(nc, [arrays], core_ids=[0])
    return r.results[0]["out_0_dram"]
```

```python
import math
from contextlib import ExitStack

import concourse.bass as bass
from concourse import mybir
from concourse.alu_op_type import AluOpType as ALU

F32 = mybir.dt.float32
F32R = mybir.dt.float32r
F16 = mybir.dt.float16
I32 = mybir.dt.int32
U32 = mybir.dt.uint32
ACT = mybir.ActivationFunctionType
AX = mybir.AxisListType


def gnn_moe_kernel(nc, x, adj, gnn_weight, gnn_bias, Wr, br, W1, b1, W2, b2, gamma, beta, out):
    P = 128
    Q, L = 4, 32
    N, D = x.shape
    E, _, F = W1.shape
    T = N // P
    QS = N // Q
    NB = T // 2
    SPLIT = 4096.0
    EPS = 1e-5
    CAPACITY = float(math.ceil(N * 1.25 / E))
    TOPK = 2
    NC = F // P
    HC = TOPK * NC
    TC = 4
    NF = T // TC
    FW = TC * P
    LAST = NB - 1
    FILL, WARM = 6, 22
    PEEL = 5

    with ExitStack() as ctx:
        def sb(name, shape, dt=F32):
            return ctx.enter_context(nc.sbuf_tensor(name, shape, dt))

        def sem(name):
            return ctx.enter_context(nc.semaphore(name))

        adj_raw = [sb(f"adj_raw{s}", [P, Q, 2, QS], I32) for s in range(2)]
        adj_pair = sb("adj_pair", [P, Q, QS, 2], F16)
        adj_t = [sb(f"adj_t{s}", [P, Q, L, 2 * L], F16) for s in range(2)]
        deg_part = [sb(f"deg_part{s}", [P, Q, 2]) for s in range(2)]
        deg_spread = [sb(f"deg_spread{s}", [P, 2, Q, L // 2, 2]) for s in range(2)]
        xs_parts = sb("xs_parts", [P, T, 2, D], F16)
        x_res = sb("x_res", [P, T, D])
        xs = sb("xs", [P, T, D])
        xn_hi = sb("xn_hi", [P, T * P], F32R)
        xn_lo = sb("xn_lo", [P, T * P], F32R)
        w1_hi = sb("w1_hi", [P, TOPK * F], F32R)
        w1_lo = sb("w1_lo", [P, TOPK * F], F32R)
        b1_rows = sb("b1_rows", [E * NC, P])
        b1_all = sb("b1_all", [P, E * NC])
        wg = sb("wg", [P, 2, D])
        bg_all = sb("bg_all", [P, D])
        wr = sb("wr", [P, E])
        br_all = sb("br_all", [P, E])
        gamma_all = sb("gamma_all", [P, D])
        beta_all = sb("beta_all", [P, D])
        ident = sb("ident", [P, P])
        ident16 = sb("ident16", [P, P], F16)
        lane_mask = sb("lane_mask", [P, L])
        split_const = sb("split_const", [P, P])
        neg_half = sb("neg_half", [P, 8])
        eps_const = sb("eps_const", [P, 2])
        ones_col = sb("ones_col", [P, 1])
        col_sum = sb("col_sum", [P, LAST])
        bn6 = sb("bn6", [P, T, 6])
        mv1 = sb("mv1", [P, T, 2])
        rstd1 = sb("rstd1", [P, T])
        bn6b = sb("bn6b", [P, 2, 6])
        x2_stage = [sb(f"x2_stage{s}", [P, 2, D]) for s in range(2)]
        xn_stage = [sb(f"xn_stage{s}", [P, 2, D]) for s in range(2)]
        mv2 = [sb(f"mv2_{s}", [P, 2, 2]) for s in range(2)]
        var2 = sb("var2", [P, 2])
        rstd2 = [sb(f"rstd2_{s}", [P, 2]) for s in range(2)]
        rdeg = [sb(f"rdeg{s}", [P, 2]) for s in range(2)]
        agg_sb = sb("agg_sb", [P, 2 * P])
        xs_t = sb("xs_t", [P, 2 * P])
        (LOGITS, NEG_MAX_1, EXP_1, SUM_1, INV_SUM, WEIGHTS_1, WR_MEAN, INV_LOAD, SCALED, NEG_MAX_2, EXP_2, SUM_2,
         WEIGHTS_2, TOP, NEG_MAX_3, EXP_3, SUM_3, SCALE, TOP_WEIGHTS, REST_SUM, WR_SUMS, WR_REST, UNREAD) = range(23)
        route = sb("route", [P, 23, E])
        top_idx = sb("top_idx", [P, 8], U32)
        b1_sel = sb("b1_sel", [P, TOPK, NC])
        b2_sel = sb("b2_sel", [P, D])
        was_pair = adj_pair[:, :, :, :].rearrange("p k s e -> p (k s e)").bitcast(F32)
        was_raw = [adj_raw[s][:, :, :, :].rearrange("p k e s -> p (k e s)").bitcast(F32) for s in range(2)]
        was_turned = adj_t[0][:, :, :, :].rearrange("p k b r -> p (k b r)").bitcast(F32)
        w2_sel = was_pair[:, 0:HC * D].rearrange("p (k d) -> p k d", k=HC)
        hid = [[was_turned[:, (s * HC + k) * FW:(s * HC + k + 1) * FW] for k in range(HC)] for s in range(2)]
        w1_all = was_raw[0][:, 0:E * F]
        w2_all = was_raw[0][:, E * F:E * F + E * NC * D].rearrange("p (k d) -> p k d", k=E * NC)
        b2_all = was_raw[0][:, E * F + E * NC * D:E * F + E * NC * D + E * D]

        def slots(n, tiles):
            return [was_raw[1][:, n * FW + s * tiles * D:n * FW + (s + 1) * tiles * D]
                    .rearrange("p (t d) -> p t d", t=tiles) for s in range(2)]
        skip, ysum, centred = slots(0, TC), slots(2, 2), slots(3, 2)
        result = [slots(4 + s, 2) for s in range(2)]
        bn6c = [sb(f"bn6c{h}", [P, 2, 6]) for h in range(2)]
        mv3 = [sb(f"mv3_{h}", [P, 2, 2]) for h in range(2)]
        var3 = [sb(f"var3_{h}", [P, 2]) for h in range(2)]
        rstd3 = [sb(f"rstd3_{h}", [P, 2]) for h in range(2)]

        bank = [ctx.enter_context(nc.psum_tensor(f"bank{i}", [P, 512], F32)) for i in range(8)]
        p_agg = [bank[0], bank[1]]
        p_xst, p_nb, p_self, p_deg = bank[2], bank[4], bank[5], bank[5][:, 2 * P:2 * P + 2]
        p_xnt = [bank[3][:, 0:2 * P], bank[6][:, 0:2 * P]]
        p_col, p_logit, p_b1 = bank[7][:, 0:1], bank[7][:, 8:8 + E], bank[7][:, P:P + E * NC]
        p_y = [[bank[4 + 2 * s + h][:, 0:2 * P] for h in range(2)] for s in range(2)]

        x_in = sem("x_in")
        weights_in = sem("weights_in")
        eps_set = sem("eps_set")
        ones_set = sem("ones_set")
        late_in = sem("late_in")
        xn2_kept = sem("xn2_kept")
        adj_in = [[[sem(f"adj_in{s}_{k}_{e}") for e in range(2)] for k in range(Q)] for s in range(2)]
        consts_done = sem("consts_done")
        pool_step = sem("pool_step")
        bn1_done = sem("bn1_done")
        stats1_done = sem("stats1_done")
        rstd1_done = sem("rstd1_done")
        norm1_done = sem("norm1_done")
        high_done = sem("high_done")
        low_done = sem("low_done")
        cast_done = sem("cast_done")
        turned = sem("turned")
        half_turned = sem("half_turned")
        spread_done = sem("spread_done")
        agg_done = sem("agg_done")
        xst_done = sem("xst_done")
        agg_copied = sem("agg_copied")
        self_done = sem("self_done")
        bias_added = sem("bias_added")
        nb_done = sem("nb_done")
        xst_copied = sem("xst_copied")
        self_added = sem("self_added")
        x2_done = sem("x2_done")
        bn2_done = sem("bn2_done")
        stats2_done = sem("stats2_done")
        var2_done = sem("var2_done")
        rstd2_done = sem("rstd2_done")
        norm2_done = sem("norm2_done")
        xnt_done = sem("xnt_done")
        xnt_copied = sem("xnt_copied")
        xn_lo_done = sem("xn_lo_done")
        w1_ready = sem("w1_ready")
        b1_ready = sem("b1_ready")
        beta_added = sem("beta_added")
        chain = sem("chain")
        col_summed = sem("col_summed")
        wr_scaled = sem("wr_scaled")
        b1_turned = sem("b1_turned")
        b1_kept = sem("b1_kept")
        logits_done = sem("logits_done")
        exp_asked = sem("exp_asked")
        exp_done = sem("exp_done")
        sel_done = sem("sel_done")
        hid_mm_done = sem("hid_mm_done")
        gelu_done = sem("gelu_done")
        y_mm_done = sem("y_mm_done")
        skip_done = sem("skip_done")
        ysum_done = sem("ysum_done")
        bn3_done = sem("bn3_done")
        stats3_done = sem("stats3_done")
        var3_done = sem("var3_done")
        rstd3_done = sem("rstd3_done")
        centred_done = sem("centred_done")
        result_done = sem("result_done")
        stored = [[sem(f"stored{s}_{h}") for h in range(2)] for s in range(2)]

        x_q = x.rearrange("(q b a) f -> q a b f", q=Q, b=T, a=L)
        out_t = out.rearrange("(q b a) f -> b q a f", q=Q, b=T, a=L)
        adj_v = adj.rearrange("(k n c e) (q s) -> n k e q c s", k=Q, n=NB, c=L, e=2, q=Q)

        block = ctx.enter_context(nc.Block())

        def x2_of(b, s):
            return x_res[:, 2 * b:2 * b + 2, :] if isinstance(b, int) and b >= LAST - 1 else x2_stage[s][:, :, :]

        def xn2_of(b, s):
            return xs[:, 2 * b:2 * b + 2, :] if isinstance(b, int) and b >= LAST - 3 else xn_stage[s][:, :, :]

        def live(b):
            return not isinstance(b, int) or 0 <= b < NB

        @block.sync
        def _(sp):
            for q in range(2):
                sp.dma_start(x_res[32 * q:32 * q + 32, :, :], x_q[q]).then_inc(x_in, 16)

            def load_adj(b, s, k):
                if not isinstance(b, int) or b >= 2:
                    sp.wait_ge(cast_done, 8 * b - 14 + 2 * k)
                for e in range(2):
                    sp.dma_start(adj_raw[s][:, k, e, :], adj_v[b, k, e]).then_inc(adj_in[s][k][e], 16)

            for b in range(2):
                for k in range(Q):
                    load_adj(b, b, k)
            with sp.Fori(2, NB - 1, 2) as b0:
                for s in range(2):
                    for k in range(Q):
                        load_adj(b0 + s, s, k)
            sp.wait_ge(cast_done, 8 * LAST)
            sp.dma_start(w1_all.rearrange("d (e f) -> d e f", e=E), W1.rearrange("e d f -> d e f"))\
              .then_inc(late_in, 16)
            sp.dma_start(w2_all, W2.rearrange("e (c f) d -> f (e c) d", c=NC)).then_inc(late_in, 16)
            sp.dma_start(b2_all, b2.rearrange("e d -> (e d)").partition_broadcast(P)).then_inc(late_in, 16)
            for p in range(2 * NF):
                s, h = p // 2 % 2, p % 2
                for t in range(2):
                    sp.wait_ge(result_done, 2 * p + t + 1)
                    sp.dma_start(out_t[2 * p + t], result[s][h][:, t, :]).then_inc(stored[s][h], 16)
            for s in range(2):
                for h in range(2):
                    sp.wait_ge(stored[s][h], 16 * NF)

        @block.scalar
        def _(act):
            for q in range(2, Q):
                act.dma_start(x_res[32 * q:32 * q + 32, :, :], x_q[q]).then_inc(x_in, 16)
            for g in range(4):
                act.wait_ge(norm1_done, 8 * (g + 1))
                act.activation(xs_parts[:, 8 * g:8 * g + 8, 0, :], xs[:, 8 * g:8 * g + 8, :], ACT.Copy)\
                   .then_inc(high_done, 1)

            def cast(s, k, e):
                act.activation(adj_pair[:, k, :, e], adj_raw[s][:, k, e, :], ACT.Copy,
                               accum_out=deg_part[s][:, k, e:e + 1]).then_inc(cast_done, 1)

            def keep_high(b, s):
                act.wait_ge(xnt_done, b + 1)
                high = xn_hi[:, bass.ds(b * 2 * P, 2 * P)]
                if isinstance(b, int) and b == LAST:
                    act.activation(high, p_xnt[s], ACT.Copy).then_inc(xnt_copied, 1)
                else:
                    act.activation(high, p_xnt[s], ACT.Copy, accum_out=col_sum[:, bass.ds(b, 1)])\
                       .then_inc(xnt_copied, 1)

            def copies(g, s):
                if live(g):
                    act.wait_ge(xst_done, g + 1)
                    if not isinstance(g, int) or g >= 1:
                        act.wait_ge(self_done, g)
                    act.activation(xs_t[:, :], p_xst[:, 0:2 * P], ACT.Copy).then_inc(xst_copied, 1)
                if live(g - 1):
                    b = g - 1
                    act.wait_ge(agg_done, b + 1)
                    if not isinstance(b, int) or b >= 1:
                        act.wait_ge(nb_done, b)
                    act.activation(agg_sb[:, :].rearrange("p (h k a) -> p k h a", h=2, k=Q),
                                   p_agg[1 - s][:, 0:2 * P]
                                   .rearrange("p (k h a) -> p k h a", k=Q, h=2), ACT.Copy).then_inc(agg_copied, 1)

            def step(g, s):
                if live(g):
                    if not isinstance(g, int) or g >= 2:
                        act.wait_ge(spread_done, 2 * g - 2)
                    for k in range(Q):
                        if not isinstance(g, int) or g >= 1:
                            act.wait_ge(turned, 4 * g - 3 + k)
                        for e in range(2):
                            act.wait_ge(adj_in[s][k][e], 8 * (g - s) + 16)
                            cast(s, k, e)
                        if isinstance(g, int) and g == LAST and k == 2:
                            copies(g, s)
                if not isinstance(g, int) or g != LAST:
                    copies(g, s)
                if live(g - 4):
                    keep_high(g - 4, s)

            for g in range(PEEL):
                step(g, g % 2)
            with act.Fori(PEEL, NB - 2, 2) as g0:
                for j in range(2):
                    step(g0 + j, (PEEL + j) % 2)
            step(LAST, LAST % 2)
            copies(NB, NB % 2)
            for b in range(NB - 4, NB):
                keep_high(b, b % 2)
            act.wait_ge(exp_asked, 1)
            act.activation(route[:, EXP_1, :], route[:, LOGITS, :], ACT.Exp, bias=route[:, NEG_MAX_1, 0:1],
                           accum_out=route[:, SUM_1, 0:1]).then_inc(exp_done, 1)
            act.wait_ge(exp_asked, 2)
            act.activation(route[:, EXP_2, :], route[:, SCALED, :], ACT.Exp, bias=route[:, NEG_MAX_2, 0:1],
                           accum_out=route[:, SUM_2, 0:1]).then_inc(exp_done, 1)
            act.wait_ge(exp_asked, 3)
            act.activation(route[:, EXP_3, 0:TOPK], route[:, TOP, 0:TOPK], ACT.Exp, bias=route[:, NEG_MAX_3, 0:1],
                           accum_out=route[:, SUM_3, 0:1]).then_inc(exp_done, 1)
            act.activation(route[:, UNREAD, 0:1], neg_half[:, 0:1], ACT.Gelu)

            def gelus(f, s):
                for k in range(HC):
                    if isinstance(f, int) and f == 0 and k % NC == 0:
                        act.wait_ge(b1_ready, k // NC + 1)
                    act.wait_ge(hid_mm_done, HC * f + k + 1)
                    if k == 0 and (not isinstance(f, int) or f >= 2):
                        act.wait_ge(y_mm_done, TC * f - TC)
                    act.activation(hid[s][k], bank[k][:, :], ACT.Gelu, bias=b1_sel[:, k // NC, k % NC:k % NC + 1])\
                       .then_inc(gelu_done, 1)
            gelus(0, 0)
            gelus(1, 1)
            with act.Fori(2, NF - 1, 2) as f0:
                gelus(f0, 0)
                gelus(f0 + 1, 1)

        @block.gpsimd
        def _(pool):
            for dst, src in (
                    (wg[:, :, :], gnn_weight.rearrange("(h f) o -> f h o", h=2)),
                    (bg_all[:, :], gnn_bias.partition_broadcast(P)),
                    (wr[:, :], Wr),
                    (br_all[:, :], br.partition_broadcast(P)),
                    (gamma_all[:, :], gamma.partition_broadcast(P)),
                    (beta_all[:, :], beta.partition_broadcast(P)),
                    (b1_rows[:, :], b1.rearrange("e (c f) -> (e c) f", c=NC))):
                pool.dma_start(dst, src).then_inc(weights_in, 16)
            pool.memset(ident[:, :], 0.0).then_inc(pool_step, 1)
            pool.memset(neg_half[:, :], -0.5).then_inc(pool_step, 1)
            pool.memset(eps_const[:, :], EPS).then_inc(eps_set, 1)
            pool.memset(ones_col[:, :], 1.0).then_inc(ones_set, 1)
            pool.memset(split_const[:, :], SPLIT).then_inc(consts_done, 1)
            pool.wait_ge(pool_step, 2)
            pool.affine_select(out=ident[:, :], in_=ident[:, :], compare_op=ALU.not_equal, fill=1.0, base=0,
                               pattern=[[-1, P]], channel_multiplier=1).then_inc(consts_done, 1)
            pool.wait_ge(consts_done, 2)
            pool.tensor_copy(ident16[:, :], ident[:, :]).then_inc(consts_done, 1)
            pool.tensor_tensor(lane_mask[:, :], ident[:, 0:L], ident[:, L:2 * L], ALU.add).then_inc(pool_step, 1)
            for q in range(2, Q):
                pool.wait_ge(pool_step, q + 1)
                pool.tensor_tensor(lane_mask[:, :], lane_mask[:, :], ident[:, q * L:q * L + L], ALU.add)\
                    .then_inc(pool_step, 1)
            pool.wait_ge(pool_step, 5)
            for g in range(4):
                r = rstd1[:, 8 * g:8 * g + 8]
                pool.wait_ge(stats1_done, 8 * (g + 1))
                pool.tensor_scalar(r, mv1[:, 8 * g:8 * g + 8, 1], EPS, None, ALU.add).then_inc(pool_step, 1)
                pool.wait_ge(pool_step, 5 + 3 * g + 1)
                pool.tensor_tensor(r, r, neg_half[:, 0:8], ALU.pow).then_inc(pool_step, 1)
                pool.wait_ge(pool_step, 5 + 3 * g + 2)
                pool.tensor_scalar(r, r, SPLIT, None, ALU.mult).then_inc(pool_step, 1)
                pool.wait_ge(pool_step, 5 + 3 * g + 3)
                pool.engine_nop().then_inc(rstd1_done, 1)

            def inverse_deviation(b, s):
                pool.wait_ge(stats2_done, 2 * b + 2)
                pool.tensor_tensor(var2[:, :], mv2[s][:, :, 1], eps_const[:, 0:2], ALU.add).then_inc(var2_done, 1)
                pool.wait_ge(var2_done, b + 1)
                pool.tensor_tensor(rstd2[s][:, :], var2[:, :], neg_half[:, 0:2], ALU.pow)\
                    .then_inc(rstd2_done, 1)

            def spread(g, s):
                pool.wait_ge(cast_done, 8 * g + 8)
                if not isinstance(g, int) or g >= 2:
                    pool.wait_ge(self_done, g - 1)
                for h in range(2):
                    pool.tensor_tensor(
                        deg_spread[s][:, h, :, :, :],
                        lane_mask[:, 16 * h:16 * h + 16].unsqueeze(1).unsqueeze(3).broadcast_to([P, Q, 16, 2]),
                        deg_part[s][:, :, :].unsqueeze(2).broadcast_to([P, Q, 16, 2]), ALU.mult)\
                        .then_inc(spread_done, 1)

            def keep(b, s):
                pool.wait_ge(norm2_done, 2 * b + 2)
                pool.tensor_tensor(x_res[:, bass.ds(2 * b, 2), :], x2_of(b, s),
                                   beta_all[:, :].unsqueeze(1).broadcast_to([P, 2, D]), ALU.add)\
                    .then_inc(beta_added, 1)
                if not isinstance(b, int) or b < LAST - 3:
                    pool.tensor_copy(xs[:, bass.ds(2 * b, 2), :], xn_stage[s][:, :, :]).then_inc(xn2_kept, 1)

            def step(g, s):
                if live(g - 3):
                    inverse_deviation(g - 3, 1 - s)
                if live(g):
                    spread(g, s)
                if live(g - 3):
                    keep(g - 3, 1 - s)

            pool.wait_ge(weights_in, 16 * 7)
            pool.wait_ge(eps_set, 1)
            for g in range(4):
                pool.wait_ge(norm1_done, 8 * (g + 1))
                pool.tensor_tensor(x_res[:, 8 * g:8 * g + 8, :], x_res[:, 8 * g:8 * g + 8, :],
                                   bg_all[:, :].unsqueeze(1).broadcast_to([P, 8, D]), ALU.add).then_inc(bias_added, 1)
            pool.wait_ge(low_done, 4)
            for g in range(PEEL):
                step(g, g % 2)
            with pool.Fori(PEEL, NB - 2, 2) as g0:
                for j in range(2):
                    step(g0 + j, (PEEL + j) % 2)
            step(LAST, LAST % 2)
            inverse_deviation(NB - 3, (NB - 3) % 2)
            for b in range(NB - 2, NB):
                inverse_deviation(b, b % 2)
                keep(b - 1, 1 - b % 2)
            keep(LAST, LAST % 2)

            def skips(f, s):
                pool.tensor_tensor(skip[s], xs[:, bass.ds(TC * f, TC), :],
                                   b2_sel[:, :].unsqueeze(1).broadcast_to([P, TC, D]), ALU.add)\
                    .then_inc(skip_done, 1)

            def rstds(p, h):
                pool.wait_ge(stats3_done, 2 * p + 2)
                pool.tensor_tensor(var3[h][:, :], mv3[h][:, :, 1], eps_const[:, :], ALU.add).then_inc(var3_done, 1)
                pool.wait_ge(var3_done, p + 1)
                pool.tensor_tensor(rstd3[h][:, :], var3[h][:, :], neg_half[:, 0:2], ALU.pow)\
                    .then_inc(rstd3_done, 1)

            pool.wait_ge(sel_done, 1)
            pool.wait_ge(xn2_kept, LAST - 3)
            pool.wait_ge(norm2_done, 2 * NB)
            skips(0, 0)
            skips(1, 1)
            with pool.Fori(0, NF - 3, 2) as f0:
                for s in range(2):
                    for h in range(2):
                        rstds((f0 + s) * 2 + h, h)
                    pool.wait_ge(ysum_done, (f0 + s) * 2 + 2)
                    skips(f0 + s + 2, s)
            for p in range(2 * NF - 4, 2 * NF):
                rstds(p, p % 2)

        @block.vector
        def _(dve):
            dve.wait_ge(x_in, 16 * Q)
            for b0 in range(0, T, 4):
                for b in range(b0, b0 + 4):
                    dve.bn_stats(bn6[:, b, :], x_res[:, b, :]).then_inc(bn1_done, 1)
                for b in range(b0, b0 + 4):
                    dve.wait_ge(bn1_done, b + 1)
                    dve.bn_aggr(mv1[:, b, :], bn6[:, b, :]).then_inc(stats1_done, 1)
            for g in range(4):
                dve.wait_ge(rstd1_done, g + 1)
                for b in range(8 * g, 8 * g + 8):
                    dve.tensor_scalar(xs[:, b, :], x_res[:, b, :], mv1[:, b, 0:1], rstd1[:, b:b + 1],
                                      ALU.subtract, ALU.mult).then_inc(norm1_done, 1)
            for g in range(4):
                dve.wait_ge(high_done, g + 1)
                dve.wait_ge(norm1_done, 8 * (g + 1))
                dve.tensor_tensor(xs_parts[:, 8 * g:8 * g + 8, 1, :], xs[:, 8 * g:8 * g + 8, :],
                                  xs_parts[:, 8 * g:8 * g + 8, 0, :], ALU.subtract).then_inc(low_done, 1)

            def turn(g, s, k):
                dve.wait_ge(cast_done, 8 * g + 2 * k + 2)
                pieces = 2 if isinstance(g, int) and g == LAST and k == Q - 1 else 1
                for i in range(pieces):
                    tiles = slice(i * T // pieces, (i + 1) * T // pieces)
                    columns = slice(i * QS // pieces, (i + 1) * QS // pieces)
                    dve.transpose(adj_t[s][:, k, tiles, :].rearrange("p b r -> p (b r)").bitcast(U32),
                                  adj_pair[:, k, columns, :].rearrange("p s e -> p (s e)").bitcast(U32))\
                       .then_inc(turned if i == pieces - 1 else half_turned, 1)

            def self_term(b, s):
                dve.wait_ge(self_done, b + 1)
                if isinstance(b, int) and b == 0:
                    dve.wait_ge(bias_added, 4)
                if not isinstance(b, int) or 2 <= b < LAST - 1:
                    dve.wait_ge(beta_added, b - 1)
                dve.scalar_tensor_tensor(x2_of(b, s), p_self[:, 0:2 * P].rearrange("p (h d) -> p h d", h=2),
                                         1.0 / SPLIT, x_res[:, bass.ds(2 * b, 2), :], ALU.mult, ALU.add)\
                   .then_inc(self_added, 1)
                dve.reciprocal(rdeg[s][:, :], p_deg[:, 0:2]).then_inc(self_added, 1)

            def residual_and_stats(b, s):
                dve.wait_ge(nb_done, b + 1)
                dve.wait_ge(self_added, 2 * b + 2)
                for h in range(2):
                    xh = x2_of(b, s)[:, h, :]
                    dve.scalar_tensor_tensor(xh, p_nb[:, h * P:h * P + P], rdeg[s][:, h:h + 1], xh,
                                             ALU.mult, ALU.add).then_inc(x2_done, 1)
                dve.wait_ge(x2_done, 2 * b + 2)
                for h in range(2):
                    dve.bn_stats(bn6b[:, h, :], x2_of(b, s)[:, h, :]).then_inc(bn2_done, 1)

            def aggregate_stats(s):
                for h in range(2):
                    dve.bn_aggr(mv2[s][:, h, :], bn6b[:, h, :]).then_inc(stats2_done, 1)

            def normalise(b, s):
                dve.wait_ge(rstd2_done, b + 1)
                dve.wait_ge(stats2_done, 2 * b + 2)
                if not isinstance(b, int) or 2 <= b < LAST - 3:
                    dve.wait_ge(xnt_done, b - 1)
                    dve.wait_ge(xn2_kept, b - 1)
                for h in range(2):
                    dve.tensor_scalar(xn2_of(b, s)[:, h, :], x2_of(b, s)[:, h, :],
                                      mv2[s][:, h, 0:1], rstd2[s][:, h:h + 1],
                                      ALU.subtract, ALU.mult).then_inc(norm2_done, 1)

            def low_part(b, s):
                dve.wait_ge(xnt_copied, b + 1)
                cols = bass.ds(b * 2 * P, 2 * P)
                dve.tensor_tensor(xn_lo[:, cols], p_xnt[s], xn_hi[:, cols].bitcast(F32), ALU.subtract)\
                   .then_inc(xn_lo_done, 1)

            def step(g, s):
                if live(g - 3):
                    dve.wait_ge(bn2_done, 2 * g - 4)
                if live(g):
                    if not isinstance(g, int) or g >= 2:
                        dve.wait_ge(agg_done, g - 1)
                    turn(g, s, 0)
                if live(g - 3):
                    aggregate_stats(1 - s)
                if live(g):
                    turn(g, s, 1)
                    turn(g, s, 2)
                if live(g - 3):
                    normalise(g - 3, 1 - s)
                if live(g - 2):
                    residual_and_stats(g - 2, s)
                if live(g):
                    turn(g, s, 3)
                if live(g - 4):
                    low_part(g - 4, s)
                if live(g - 1):
                    self_term(g - 1, 1 - s)

            for g in range(PEEL):
                step(g, g % 2)
            with dve.Fori(PEEL, NB - 2, 2) as g0:
                for j in range(2):
                    step(g0 + j, (PEEL + j) % 2)
            step(LAST, LAST % 2)
            for b in range(NB - 3, NB):
                s = b % 2
                dve.wait_ge(bn2_done, 2 * b + 2)
                aggregate_stats(s)
                if b + 1 == LAST:
                    normalise(b, s)
                    self_term(LAST, LAST % 2)
                    residual_and_stats(LAST, LAST % 2)
                elif b + 1 < LAST:
                    residual_and_stats(b + 1, 1 - s)
                    normalise(b, s)
                else:
                    for low in range(NB - 4, NB - 2):
                        low_part(low, low % 2)
                    normalise(b, s)

            links = [0]

            def link(ins):
                links[0] += 1
                ins.then_inc(chain, 1)
                dve.wait_ge(chain, links[0])

            def row(i, n=E):
                return route[:, i, 0:n]

            dve.wait_ge(weights_in, 16 * 7)
            dve.wait_ge(b1_turned, 1)
            link(dve.tensor_scalar(row(WR_MEAN), wr[:, :], 1.0 / (N * SPLIT), None, ALU.mult))
            dve.wait_ge(xnt_copied, LAST)
            link(dve.reduce_sum(row(REST_SUM, 1), col_sum[:, :], AX.X))
            link(dve.tensor_scalar(row(WR_REST), row(WR_MEAN), row(REST_SUM, 1), None, ALU.mult))
            dve.wait_ge(col_summed, 1)
            dve.scalar_tensor_tensor(row(WR_SUMS), row(WR_MEAN), p_col, row(WR_REST), ALU.mult, ALU.add).then_inc(wr_scaled, 1)
            dve.wait_ge(logits_done, 1)
            link(dve.tensor_tensor(row(LOGITS), p_logit, br_all[:, :], ALU.add))

            dve.reduce_max(row(NEG_MAX_1, 1), row(LOGITS), AX.X, negate=True).then_inc(exp_asked, 1)
            low_part(NB - 2, NB % 2)
            dve.tensor_copy(b1_all[:, :], p_b1).then_inc(b1_kept, 1)
            dve.wait_ge(exp_done, 1)
            link(dve.reciprocal(row(INV_SUM, 1), row(SUM_1, 1)))
            link(dve.tensor_scalar(row(WEIGHTS_1), row(EXP_1), row(INV_SUM, 1), None, ALU.mult))
            link(dve.reciprocal(row(INV_LOAD), row(WEIGHTS_1)))
            link(dve.tensor_scalar(row(SCALE), row(INV_LOAD), CAPACITY / N, 1.0, ALU.mult, ALU.min))
            link(dve.tensor_tensor(row(SCALED), row(WEIGHTS_1), row(SCALE), ALU.mult))
            dve.reduce_max(row(NEG_MAX_2, 1), row(SCALED), AX.X, negate=True).then_inc(exp_asked, 1)
            low_part(LAST, LAST % 2)
            dve.wait_ge(exp_done, 2)
            link(dve.reciprocal(row(INV_SUM, 1), row(SUM_2, 1)))
            link(dve.tensor_scalar(row(WEIGHTS_2), row(EXP_2), row(INV_SUM, 1), None, ALU.mult))
            link(dve.max(row(TOP), row(WEIGHTS_2)))
            link(dve.max_index(top_idx[:, :], row(TOP), row(WEIGHTS_2)))
            dve.tensor_scalar(row(NEG_MAX_3, 1), row(TOP, 1), -1.0, None, ALU.mult).then_inc(exp_asked, 1)
            dve.wait_ge(late_in, 48)
            dve.wait_ge(b1_kept, 1)
            chosen = []
            for k in range(TOPK):
                chosen.append(dve.value_load(top_idx[0:1, k:k + 1], min_val=0, max_val=E - 1))
                dve.tensor_copy(w1_hi[:, k * F:k * F + F], w1_all[:, bass.ds(chosen[k] * F, F)]).then_inc(w1_ready, 1)
                dve.tensor_copy(b1_sel[:, k, :], b1_all[:, bass.ds(chosen[k] * NC, NC)]).then_inc(b1_ready, 1)
                dve.wait_ge(w1_ready, 2 * k + 1)
                dve.tensor_tensor(w1_lo[:, k * F:k * F + F], w1_all[:, bass.ds(chosen[k] * F, F)],
                                  w1_hi[:, k * F:k * F + F].bitcast(F32), ALU.subtract).then_inc(w1_ready, 1)
            dve.wait_ge(exp_done, 3)
            link(dve.reciprocal(row(INV_SUM, 1), row(SUM_3, 1)))
            link(dve.tensor_scalar(row(TOP_WEIGHTS, TOPK), row(EXP_3, TOPK), row(INV_SUM, 1), None, ALU.mult))
            for k in range(TOPK):
                dve.tensor_scalar(w2_sel[:, NC * k:NC * k + NC, :], w2_all[:, bass.ds(chosen[k] * NC, NC), :],
                                  route[:, TOP_WEIGHTS, k:k + 1], None, ALU.mult)
            link(dve.tensor_scalar(b2_sel[:, :], b2_all[:, bass.ds(chosen[0] * D, D)], route[:, TOP_WEIGHTS, 0:1], None,
                                   ALU.mult))
            dve.scalar_tensor_tensor(b2_sel[:, :], b2_all[:, bass.ds(chosen[1] * D, D)], route[:, TOP_WEIGHTS, 1:2],
                                     b2_sel[:, :], ALU.mult, ALU.add).then_inc(sel_done, 1)

            def add_up(f, s, h):
                dve.wait_ge(y_mm_done, f * TC + 2 * h + 2)
                dve.wait_ge(skip_done, f + 1)
                dve.tensor_tensor(ysum[h], p_y[s][h].rearrange("p (t d) -> p t d", t=2), skip[s][:, 2 * h:2 * h + 2, :],
                                  ALU.add).then_inc(ysum_done, 1)

            def statistics(f, h):
                dve.wait_ge(ysum_done, f * 2 + h + 1)
                for t in range(2):
                    dve.bn_stats(bn6c[h][:, t, :], ysum[h][:, t, :]).then_inc(bn3_done, 1)

            def centre(f, h):
                for t in range(2):
                    dve.bn_aggr(mv3[h][:, t, :], bn6c[h][:, t, :]).then_inc(stats3_done, 1)
                dve.wait_ge(stats3_done, f * 4 + 2 * h + 2)
                for t in range(2):
                    dve.scalar_tensor_tensor(centred[h][:, t, :], ysum[h][:, t, :], mv3[h][:, t, 0:1],
                                             gamma_all[:, :], ALU.subtract, ALU.mult).then_inc(centred_done, 1)

            def emit(f, s, h, t):
                dve.wait_ge(rstd3_done, f * 2 + h + 1)
                dve.wait_ge(centred_done, f * 4 + 2 * h + 2)
                if not isinstance(f, int) or f >= 2:
                    dve.wait_ge(stored[s][h], (f - s) * 16)
                dve.scalar_tensor_tensor(result[s][h][:, t, :], centred[h][:, t, :], rstd3[h][:, t:t + 1],
                                         x_res[:, bass.ds(f * TC + (2 * h + t), 1), :].rearrange("p o d -> p (o d)"),
                                         ALU.mult, ALU.add).then_inc(result_done, 1)

            def pipelined(f, s, h):
                before = (f, s, 0) if h == 1 else (f - 1, 1 - s, 1)
                add_up(f, s, h)
                statistics(f, h)
                if h == 1 or not isinstance(f, int) or f >= 1:
                    emit(*before, 0)
                dve.wait_ge(bn3_done, f * 4 + 2 * h + 2)
                if h == 1 or not isinstance(f, int) or f >= 1:
                    emit(*before, 1)
                centre(f, h)

            dve.wait_ge(beta_added, NB)
            for f in range(2):
                for h in range(2):
                    pipelined(f, f, h)
            with dve.Fori(2, NF - 1, 2) as f0:
                for s in range(2):
                    for h in range(2):
                        pipelined(f0 + s, s, h)
            emit(NF - 1, 1, 1, 0)
            emit(NF - 1, 1, 1, 1)

        @block.tensor
        def _(pe):
            pe.wait_ge(weights_in, 16 * 7)
            pe.wait_ge(consts_done, 3)
            pe.wait_ge(ones_set, 1)
            pe.transpose(p_b1, b1_rows[:, :], ident[0:E * NC, 0:E * NC]).then_inc(b1_turned, 1)

            def aggregate(g, s, tiles, k0=0, k1=Q):
                for b in tiles:
                    if isinstance(g, int) and g == 0 and b % 8 == 0:
                        pe.wait_ge(low_done, b // 8 + 1)
                    for part in range(2):
                        mm = pe.matmul(p_agg[s][:, 2 * L * k0:2 * L * k1].rearrange("p (k r) -> p k r", k=k1 - k0),
                                       xs_parts[:, b, part, :], adj_t[s][:, k0:k1, b, :],
                                       start=(b == 0 and part == 0), stop=(b == T - 1 and part == 1))
                return mm

            def turn_xs(g):
                if not isinstance(g, int) or g >= 1:
                    pe.wait_ge(xst_copied, g)
                for h in range(2):
                    for part in range(2):
                        mm = pe.matmul(p_xst[:, h * P:h * P + P],
                                       xs_parts[:, bass.ds(2 * g + h, 1), part, :].rearrange("p o d -> p (o d)"),
                                       ident16[:, :], start=(part == 0), stop=(part == 1))
                mm.then_inc(xst_done, 1)

            def own_part(g, s):
                pe.wait_ge(xst_copied, g + 1)
                if not isinstance(g, int) or g >= 1:
                    pe.wait_ge(self_added, 2 * g)
                for h in range(2):
                    pe.matmul(p_self[:, h * P:h * P + P], xs_t[:, h * P:h * P + P], wg[:, 1, :],
                              start=True, stop=True)
                pe.wait_ge(spread_done, 2 * g + 2)
                for h in range(2):
                    mm = pe.matmul(p_deg[:, h:h + 1], deg_spread[s][:, h, :, :, :].rearrange("p k a e -> p (k a e)"),
                                   split_const[:, 0:1], start=True, stop=True)
                mm.then_inc(self_done, 1)

            def neighbour_part(b):
                pe.wait_ge(agg_copied, b + 1)
                if not isinstance(b, int) or b >= 1:
                    pe.wait_ge(x2_done, 2 * b)
                for h in range(2):
                    mm = pe.matmul(p_nb[:, h * P:h * P + P], agg_sb[:, h * P:h * P + P], wg[:, 0, :],
                                   start=True, stop=True)
                mm.then_inc(nb_done, 1)

            def sum_up_last():
                pe.wait_ge(norm2_done, 2 * NB)
                for h in range(2):
                    mm = pe.matmul(p_col, xn2_of(LAST, 1)[:, h, :], ones_col[:, :], start=(h == 0), stop=(h == 1))
                mm.then_inc(col_summed, 1)

            def keep_busy(products):
                for i in range(products):
                    pe.matmul(bank[0][:, 0:2 * P], xs_parts[:, i, 0, :], xs_parts[:, i, :, :], start=True, stop=True)

            def turn_xn(b, s):
                pe.wait_ge(norm2_done, 2 * b + 2)
                if not isinstance(b, int) or b >= 2:
                    pe.wait_ge(xn_lo_done, b - 1)
                for h in range(2):
                    mm = pe.transpose(p_xnt[s][:, h * P:h * P + P], xn2_of(b, s)[:, h, :], ident[:, :])
                mm.then_inc(xnt_done, 1)

            def step(g, s):
                cut = isinstance(g, int) and LAST - 2 <= g <= LAST
                if live(g):
                    pe.wait_ge(turned, 4 * g + (2 if cut else 4))
                    if not isinstance(g, int) or g >= 2:
                        pe.wait_ge(agg_copied, g - 1)
                    if cut:
                        aggregate(g, s, range(T), 0, 2)
                    else:
                        aggregate(g, s, range(T // 2))
                if live(g - 1):
                    neighbour_part(g - 1)
                if live(g - 3) and (not isinstance(g, int) or g < LAST):
                    turn_xn(g - 3, 1 - s)
                if live(g):
                    if isinstance(g, int) and g == LAST:
                        pe.wait_ge(turned, 4 * g + 3)
                        aggregate(g, s, range(T), 2, 3)
                    if not isinstance(g, int) or g < LAST:
                        own_part(g, s)
                        turn_xs(g + 1)
                    if isinstance(g, int) and g == LAST:
                        pe.wait_ge(half_turned, 1)
                        aggregate(g, s, range(T // 2), 3, 4)
                        pe.wait_ge(turned, 4 * g + 4)
                        aggregate(g, s, range(T // 2, T), 3, 4).then_inc(agg_done, 1)
                    elif cut:
                        pe.wait_ge(turned, 4 * g + 4)
                        aggregate(g, s, range(T), 2, 4).then_inc(agg_done, 1)
                    else:
                        aggregate(g, s, range(T // 2, T)).then_inc(agg_done, 1)

            pe.wait_ge(low_done, 1)
            turn_xs(0)
            for g in range(PEEL):
                step(g, g % 2)
            with pe.Fori(PEEL, NB - 4, 2) as g0:
                for j in range(2):
                    step(g0 + j, (PEEL + j) % 2)
            for g in range(NB - 3, NB):
                step(g, g % 2)
            own_part(LAST, LAST % 2)
            neighbour_part(LAST)
            for b in range(NB - 4, NB - 2):
                turn_xn(b, b % 2)
            keep_busy(FILL)
            turn_xn(NB - 2, NB % 2)
            sum_up_last()
            turn_xn(LAST, LAST % 2)
            pe.wait_ge(wr_scaled, 1)
            pe.matmul(p_logit, split_const[:, :], route[:, WR_SUMS, :], start=True, stop=True).then_inc(logits_done, 1)

            keep_busy(WARM)
            pe.wait_ge(xn_lo_done, NB)

            def hidden(f, j):
                for k in range(j * NC, j * NC + NC):
                    if isinstance(f, int) and f == 0 and k % NC == 0:
                        pe.wait_ge(w1_ready, 2 * j + 2)
                    if not isinstance(f, int) or f >= 1:
                        pe.wait_ge(gelu_done, HC * f - HC + k + 1)
                    ks, cols = slice(k * P, k * P + P), bass.ds(f * FW, FW)
                    pe.matmul(bank[k][:, :], w1_hi[:, ks], xn_hi[:, cols], start=True, stop=False)
                    pe.matmul(bank[k][:, :], w1_hi[:, ks], xn_lo[:, cols], start=False, stop=False)
                    pe.matmul(bank[k][:, :], w1_lo[:, ks], xn_hi[:, cols], start=False, stop=True)\
                        .then_inc(hid_mm_done, 1)

            def combine(f, s, h):
                if not isinstance(f, int) or f >= 2:
                    pe.wait_ge(ysum_done, f * 2 + (h - 3))
                pe.wait_ge(gelu_done, HC * f + HC)
                for t in range(2 * h, 2 * h + 2):
                    for k in range(HC):
                        mm = pe.matmul(p_y[s][h][:, t % 2 * P:t % 2 * P + P], hid[s][k][:, t * P:t * P + P],
                                       w2_sel[:, k, :], start=(k == 0), stop=(k == HC - 1))
                    mm.then_inc(y_mm_done, 1)

            def pipelined(f, s):
                for h in range(2):
                    hidden(f + 1, h)
                    combine(f, s, h)

            for j in range(TOPK):
                hidden(0, j)
            hidden(1, 0)
            hidden(1, 1)
            pe.wait_ge(sel_done, 1)
            combine(0, 0, 0)
            combine(0, 0, 1)
            pipelined(1, 1)
            pipelined(2, 0)
            with pe.Fori(3, NF - 2, 2) as f0:
                pipelined(f0, 1)
                pipelined(f0 + 1, 0)
            combine(NF - 1, 1, 0)
            combine(NF - 1, 1, 1)


_INS = ['x', 'adj', 'L0_gnn_weight', 'L0_gnn_bias', 'L0_ffn_Wr', 'L0_ffn_br', 'L0_ffn_W1', 'L0_ffn_b1',
        'L0_ffn_W2', 'L0_ffn_b2', 'L0_ffn_gamma', 'L0_ffn_beta']
_OUTS = [((4096, 128), 'float32')]


def kernel(**inputs):
    import numpy as _np
    import concourse.bacc as _bacc
    from concourse import mybir as _mybir
    from concourse.bass_utils import run_bass_kernel_spmd as _run

    nc = _bacc.Bacc("TRN2", target_bir_lowering=False, num_devices=1, dynamic_dma_scratch_size=8192)
    arrays, args = {}, []
    for name in _INS:
        a = _np.ascontiguousarray(inputs[name])
        arrays[f"in_{name}_dram"] = a
        args.append(nc.dram_tensor(f"in_{name}_dram", a.shape, _mybir.dt.from_np(a.dtype), kind="ExternalInput").ap())
    for i, (shape, dtype) in enumerate(_OUTS):
        dt = _mybir.dt.from_np(_np.dtype(dtype))
        args.append(nc.dram_tensor(f"out_{i}_dram", shape, dt, kind="ExternalOutput").ap())
    gnn_moe_kernel(nc, *args)
    r = _run(nc, [arrays], core_ids=[0])
    return r.results[0]["out_0_dram"]
```
